# Optimizing a Trainium2 kernel written in Bass

```python
import numpy as np
import jax
import jax.numpy as jnp

def _softmax(x, axis=-1):
    return jax.nn.softmax(x, axis=axis)

def _gelu(x):
    return jax.nn.gelu(x, approximate=True)

def _silu(x):
    return jax.nn.silu(x)

def _sigmoid(x):
    return jax.nn.sigmoid(x)

def _layernorm(x, axis=-1, eps=1e-05):
    m = jnp.mean(x, axis=axis, keepdims=True)
    v = jnp.var(x, axis=axis, keepdims=True)
    return (x - m) / jnp.sqrt(v + eps)

def _scatter_add(tgt, idx, src, axis=0):
    return tgt.at[idx].add(src)

def _segment_sum(src, seg, n):
    return jax.ops.segment_sum(src, seg, n)
kernel_name = 'mk_flamingo_gated_d2_seqx_r4_624281'

def setup_inputs(seed: int=0):
    np.random.seed(seed)
    _w = jnp.asarray

    def _rec_inputs():
        import jax
        import jax.numpy as jnp
        _rk = jax.random.key(seed)
        x = -1.394e-06 + 0.9999 * jax.random.normal(jax.random.fold_in(_rk, 1), (2, 1024, 256), jnp.float32)
        _lenS = 1024 - jax.random.randint(jax.random.fold_in(_rk, 7), (2,), 0, max(1, 1024 // 4) + 1, jnp.int32)
        _lenS2 = 77 - jax.random.randint(jax.random.fold_in(_rk, 8), (2,), 0, max(1, 77 // 4) + 1, jnp.int32)
        _ctx_1024P = jax.random.normal(jax.random.fold_in(_rk, 11), (2, 16, 256), jnp.float32)
        _ctx_1024c = jax.random.dirichlet(jax.random.fold_in(_rk, 511), 0.3 * jnp.ones((16,), jnp.float32), (2, 77))
        _ctx_1024t = jnp.einsum('bsk,bkd->bsd', _ctx_1024c, _ctx_1024P)
        _ctx_1024t = _ctx_1024t * jax.lax.rsqrt(jnp.mean(jnp.square(_ctx_1024t)) + 1e-12) * 0.953939
        ctx_1024 = -0.000292821 + 1.00034 * (_ctx_1024t + 0.3 * jax.random.normal(jax.random.fold_in(_rk, 611), (2, 77, 256), jnp.float32))
        _g = jax.random.normal(jax.random.fold_in(_rk, 9001), (2, 2), jnp.float32)
        _g = jnp.sign(_g) * jnp.maximum(jnp.abs(_g), 1.0) + (_g == 0) * 1.0
        g_xattn = _g[0]
        g_ffn = _g[1]
        return (x, ctx_1024, g_xattn, g_ffn)
    x, ctx_1024, g_xattn, g_ffn = _rec_inputs()

    def _L0_xattn_setup():
        import jax, jax.numpy as jnp
        import numpy as np
        B, N, T = (2, 512, 512)
        ENC, DEC, HID = (256, 256, 256)
        HEADS = 16
        DH = HID // HEADS
        HALF = DH // 2
        LAMBDA_INIT = 0.8
        key = jax.random.key(seed)
        ks = jax.random.split(key, 9)
        s = 0.02
        return {'encoder_feature': jax.random.normal(ks[0], (B, N, ENC), jnp.float32), 'decoder_feature': jax.random.normal(ks[1], (B, T, DEC), jnp.float32), 'Wq': jax.random.normal(ks[2], (HID, DEC), jnp.float32) * s, 'Wk': jax.random.normal(ks[3], (HID, ENC), jnp.float32) * s, 'Wv': jax.random.normal(ks[4], (HID, ENC), jnp.float32) * s, 'lambda_q1': jax.random.normal(ks[5], (HALF,), jnp.float32) * 0.1, 'lambda_q2': jax.random.normal(ks[6], (HALF,), jnp.float32) * 0.1, 'lambda_k1': jax.random.normal(ks[7], (HALF,), jnp.float32) * 0.1, 'lambda_k2': jax.random.normal(ks[8], (HALF,), jnp.float32) * 0.1}
    _L0_xattn_all = _L0_xattn_setup()
    _L0_xattn_in = {k: v for k, v in _L0_xattn_all.items() if k in ('Wq', 'Wk', 'Wv', 'lambda_q1', 'lambda_q2', 'lambda_k1', 'lambda_k2')}
    del _L0_xattn_all

    def _L0_ffn_setup():
        import jax, jax.numpy as jnp
        import numpy as np
        D_MODEL = 256
        D_FF = 1024
        N_ZONES = 8
        TOP_K = 3
        ROUTER_H = 64
        BATCH = 16
        SEQ = 512
        key = jax.random.key(seed)
        ks = jax.random.split(key, 8)
        s = lambda *dims: 1.0 / np.sqrt(dims[-2] if len(dims) > 1 else dims[-1])
        x = jax.random.normal(ks[0], (BATCH, SEQ, D_MODEL), dtype=jnp.float32)
        W1 = jax.random.normal(ks[1], (D_MODEL, ROUTER_H), dtype=jnp.float32) / np.sqrt(D_MODEL)
        b1 = jnp.zeros((ROUTER_H,), dtype=jnp.float32)
        W2 = jax.random.normal(ks[2], (ROUTER_H, N_ZONES), dtype=jnp.float32) / np.sqrt(ROUTER_H)
        b2 = jnp.zeros((N_ZONES,), dtype=jnp.float32)
        Wa = jax.random.normal(ks[3], (N_ZONES, D_MODEL, D_FF), dtype=jnp.float32) / np.sqrt(D_MODEL)
        Wb = jax.random.normal(ks[4], (N_ZONES, D_FF, D_MODEL), dtype=jnp.float32) / np.sqrt(D_FF)
        return {'x': x, 'W1': W1, 'b1': b1, 'W2': W2, 'b2': b2, 'Wa': Wa, 'Wb': Wb}
    _L0_ffn_all = _L0_ffn_setup()
    _L0_ffn_in = {k: v for k, v in _L0_ffn_all.items() if k in ('W1', 'b1', 'W2', 'b2', 'Wa', 'Wb')}
    del _L0_ffn_all

    def _L1_xattn_setup():
        import jax, jax.numpy as jnp
        import numpy as np
        N_HEAD = 16
        D_MODEL = 256
        D_K = D_MODEL // N_HEAD

        def _split_heads(x, B):
            return x.reshape(B, -1, N_HEAD, D_K).transpose(0, 2, 1, 3)
        key = jax.random.key(seed)
        ks = jax.random.split(key, 7)
        B, S = (4, 512)
        scale = 1.0 / np.sqrt(D_MODEL)
        return {'Q': jax.random.normal(ks[0], (B, S, D_MODEL), jnp.float32), 'K': jax.random.normal(ks[1], (B, S, D_MODEL), jnp.float32), 'V': jax.random.normal(ks[2], (B, S, D_MODEL), jnp.float32), 'Wq': jax.random.normal(ks[3], (D_MODEL, D_MODEL), jnp.float32) * scale, 'bq': jnp.zeros((D_MODEL,), jnp.float32), 'Wo': jax.random.normal(ks[4], (D_MODEL, D_MODEL), jnp.float32) * scale, 'bo': jnp.zeros((D_MODEL,), jnp.float32)}
    _L1_xattn_all = _L1_xattn_setup()
    _L1_xattn_in = {k: v for k, v in _L1_xattn_all.items() if k in ('Wq', 'bq', 'Wo', 'bo')}
    del _L1_xattn_all

    def _L1_ffn_setup():
        import jax, jax.numpy as jnp
        import numpy as np
        DIM = 256
        HIDDEN = 768
        SCALE = 1.0 / 127.0

        def _dequant(w_int, dtype):
            return w_int.astype(dtype) * jnp.asarray(SCALE, dtype)
        key = jax.random.key(seed)
        k_x, k_g, k_u, k_d = jax.random.split(key, 4)
        x = jax.random.normal(k_x, (4, 512, DIM), dtype=jnp.float32)
        w_gate = jax.random.randint(k_g, (HIDDEN, DIM), -127, 128, dtype=jnp.int32)
        w_up = jax.random.randint(k_u, (HIDDEN, DIM), -127, 128, dtype=jnp.int32)
        w_down = jax.random.randint(k_d, (DIM, HIDDEN), -127, 128, dtype=jnp.int32)
        return {'x': x, 'w_gate': w_gate, 'w_up': w_up, 'w_down': w_down}
    _L1_ffn_all = _L1_ffn_setup()
    _L1_ffn_in = {k: v for k, v in _L1_ffn_all.items() if k in ('w_gate', 'w_up', 'w_down')}
    del _L1_ffn_all
    return {'x': x, 'ctx_1024': ctx_1024, 'g_xattn': g_xattn, 'g_ffn': g_ffn, 'L0_xattn_Wq': _L0_xattn_in['Wq'], 'L0_xattn_Wk': _L0_xattn_in['Wk'], 'L0_xattn_Wv': _L0_xattn_in['Wv'], 'L0_xattn_lambda_q1': _L0_xattn_in['lambda_q1'], 'L0_xattn_lambda_q2': _L0_xattn_in['lambda_q2'], 'L0_xattn_lambda_k1': _L0_xattn_in['lambda_k1'], 'L0_xattn_lambda_k2': _L0_xattn_in['lambda_k2'], 'L0_ffn_W1': _L0_ffn_in['W1'], 'L0_ffn_b1': _L0_ffn_in['b1'], 'L0_ffn_W2': _L0_ffn_in['W2'], 'L0_ffn_b2': _L0_ffn_in['b2'], 'L0_ffn_Wa': _L0_ffn_in['Wa'], 'L0_ffn_Wb': _L0_ffn_in['Wb'], 'L1_xattn_Wq': _L1_xattn_in['Wq'], 'L1_xattn_bq': _L1_xattn_in['bq'], 'L1_xattn_Wo': _L1_xattn_in['Wo'], 'L1_xattn_bo': _L1_xattn_in['bo'], 'L1_ffn_w_gate': _L1_ffn_in['w_gate'], 'L1_ffn_w_up': _L1_ffn_in['w_up'], 'L1_ffn_w_down': _L1_ffn_in['w_down']}

def reference(x, ctx_1024, g_xattn, g_ffn, L0_xattn_Wq, L0_xattn_Wk, L0_xattn_Wv, L0_xattn_lambda_q1, L0_xattn_lambda_q2, L0_xattn_lambda_k1, L0_xattn_lambda_k2, L0_ffn_W1, L0_ffn_b1, L0_ffn_W2, L0_ffn_b2, L0_ffn_Wa, L0_ffn_Wb, L1_xattn_Wq, L1_xattn_bq, L1_xattn_Wo, L1_xattn_bo, L1_ffn_w_gate, L1_ffn_w_up, L1_ffn_w_down):
    import jax
    import jax.numpy as jnp

    def _L0_xattn_ref(encoder_feature, decoder_feature, Wq, Wk, Wv, lambda_q1, lambda_q2, lambda_k1, lambda_k2):
        import jax, jax.numpy as jnp
        import numpy as np
        B, N, T = (2, 512, 512)
        ENC, DEC, HID = (256, 256, 256)
        HEADS = 16
        DH = HID // HEADS
        HALF = DH // 2
        LAMBDA_INIT = 0.8
        b, n, _ = encoder_feature.shape
        _, t, _ = decoder_feature.shape
        hid = Wq.shape[0]
        dh = hid // HEADS
        half = dh // 2
        q = decoder_feature @ Wq.T
        k = encoder_feature @ Wk.T
        v = encoder_feature @ Wv.T
        q = q.reshape(b, t, 2 * HEADS, half).transpose(0, 2, 1, 3)
        k = k.reshape(b, n, 2 * HEADS, half).transpose(0, 2, 1, 3)
        v = v.reshape(b, n, HEADS, dh).transpose(0, 2, 1, 3)
        lam = jnp.exp(jnp.sum(lambda_q1 * lambda_k1)) - jnp.exp(jnp.sum(lambda_q2 * lambda_k2)) + LAMBDA_INIT
        scale = 1.0 / jnp.sqrt(jnp.float32(half))
        att = jax.nn.softmax(jnp.einsum('bhtd,bhnd->bhtn', q, k) * scale, axis=-1)
        att = att.reshape(b, HEADS, 2, t, n)
        att = att[:, :, 0] - lam * att[:, :, 1]
        out = jnp.einsum('bhtn,bhnd->bhtd', att, v)
        return out.transpose(0, 2, 1, 3).reshape(b, t, hid)

    def _L0_ffn_ref(x, W1, b1, W2, b2, Wa, Wb):
        import jax, jax.numpy as jnp
        import numpy as np
        D_MODEL = 256
        D_FF = 1024
        N_ZONES = 8
        TOP_K = 3
        ROUTER_H = 64
        BATCH = 16
        SEQ = 512
        pooled = x.mean(axis=1)
        h = jnp.tanh(pooled @ W1 + b1)
        logits = h @ W2 + b2
        probs = jax.nn.softmax(logits, axis=-1)
        top_p, top_i = jax.lax.top_k(probs, TOP_K)
        top_w = top_p / top_p.sum(axis=-1, keepdims=True)
        onehot = jax.nn.one_hot(top_i, N_ZONES, dtype=x.dtype)
        w = jnp.einsum('bk,bke->be', top_w, onehot)
        zone_outputs = jnp.zeros_like(x)
        for e in range(N_ZONES):
            z = jax.nn.gelu(x @ Wa[e]) @ Wb[e]
            zone_outputs = zone_outputs + z * w[:, e, None, None]
        return x + zone_outputs

    def _L1_xattn_ref(Q, K, V, Wq, bq, Wo, bo):
        import jax, jax.numpy as jnp
        import numpy as np
        N_HEAD = 16
        D_MODEL = 256
        D_K = D_MODEL // N_HEAD

        def _split_heads(x, B):
            return x.reshape(B, -1, N_HEAD, D_K).transpose(0, 2, 1, 3)
        B = Q.shape[0]
        q = _split_heads(Q @ Wq + bq, B)
        k = _split_heads(K @ Wq + bq, B)
        v = _split_heads(V @ Wq + bq, B)
        scores = jnp.einsum('bhqd,bhkd->bhqk', q, k) / jnp.sqrt(jnp.asarray(D_K, q.dtype))
        attn = jax.nn.softmax(scores, axis=-1)
        out = jnp.einsum('bhqk,bhkd->bhqd', attn, v)
        out = out.transpose(0, 2, 1, 3).reshape(B, -1, D_MODEL)
        return out @ Wo + bo

    def _L1_ffn_ref(x, w_gate, w_up, w_down):
        import jax, jax.numpy as jnp
        import numpy as np
        DIM = 256
        HIDDEN = 768
        SCALE = 1.0 / 127.0

        def _dequant(w_int, dtype):
            return w_int.astype(dtype) * jnp.asarray(SCALE, dtype)
        wg = _dequant(w_gate, x.dtype)
        wu = _dequant(w_up, x.dtype)
        wd = _dequant(w_down, x.dtype)
        gate = jnp.einsum('bsd,hd->bsh', x, wg)
        up = jnp.einsum('bsd,hd->bsh', x, wu)
        h = jax.nn.silu(gate) * up
        return jnp.einsum('bsh,dh->bsd', h, wd)
    x = x + jnp.tanh(g_xattn[0]) * _L0_xattn_ref(ctx_1024, _layernorm(x, axis=-1), L0_xattn_Wq, L0_xattn_Wk, L0_xattn_Wv, L0_xattn_lambda_q1, L0_xattn_lambda_q2, L0_xattn_lambda_k1, L0_xattn_lambda_k2)
    x = x + jnp.tanh(g_ffn[0]) * _L0_ffn_ref(_layernorm(x, axis=-1), L0_ffn_W1, L0_ffn_b1, L0_ffn_W2, L0_ffn_b2, L0_ffn_Wa, L0_ffn_Wb)
    x = x + jnp.tanh(g_xattn[1]) * _L1_xattn_ref(_layernorm(x, axis=-1), ctx_1024, ctx_1024, L1_xattn_Wq, L1_xattn_bq, L1_xattn_Wo, L1_xattn_bo)
    x = x + jnp.tanh(g_ffn[1]) * _L1_ffn_ref(_layernorm(x, axis=-1), L1_ffn_w_gate, L1_ffn_w_up, L1_ffn_w_down)
    return x

_drawn_inputs = setup_inputs


def setup_inputs(seed=0):
    import zlib

    import numpy as np

    out = dict(_drawn_inputs(seed))
    spreads = {'g_ffn': (-1.0, 0.2),
     'L0_ffn_b1': (0.0, 0.1),
     'L0_ffn_b2': (0.0, 0.1),
     'L1_xattn_bq': (0.0, 0.1),
     'L1_xattn_bo': (0.0, 0.1)}
    factors = {'L0_xattn_Wq': 8.0,
     'L0_xattn_Wk': 8.0,
     'L0_xattn_lambda_q1': 8.0,
     'L0_xattn_lambda_q2': 8.0,
     'L0_xattn_lambda_k1': 8.0,
     'L0_xattn_lambda_k2': 6.589}
    for name, (base, spread) in spreads.items():
        noise = np.random.default_rng([zlib.crc32(name.encode()), seed]).standard_normal(out[name].shape)
        drawn = base * np.exp(spread * noise) if base else spread * noise
        out[name] = jnp.asarray(drawn.astype(out[name].dtype))
    for name, factor in factors.items():
        out[name] = (out[name] * factor).astype(out[name].dtype)
    return out
```

```python
from contextlib import ExitStack

import concourse.bass as bass
from concourse import mybir

F32 = mybir.dt.float32
F32R = mybir.dt.float32r
I32 = mybir.dt.int32
U32 = mybir.dt.uint32
ALU = mybir.AluOpType
ACT = mybir.ActivationFunctionType
AX_X = mybir.AxisListType.X

P = 128
B, T, D, S = 2, 1024, 256, 77
NT = 512
J = B * T // NT
TT = NT // P
KC = D // P
G = D // 32
HEADS = (32, 16)
NS = tuple(h // G for h in HEADS)
DV = 16
SCALE = (8 ** -0.5, 16 ** -0.5)
LAMBDA_INIT = 0.8
EPS = 1e-5
NZ, TOPK, RH, FF = 8, 3, 64, 1024
FC = FF // P
Z = B * TOPK
HID = 768
HC = HID // P
DEQ = 1.0 / 127.0
ATT0, FFN0, ATT1, FFN1 = range(4)
SMALL = 15
LAG = 2
ROWS = 96


def weave(main, side):
    out = []
    for n, step in enumerate(main):
        out.append(step)
        out += side.get(n, [])
    return out


def spread(side, steps, first, last):
    for i, s in enumerate(steps):
        side.setdefault(first + i * (last - first) // len(steps), []).append(s)


def plan():
    def units(a):
        return 8 if a == 0 else 4

    def maxima(a, j):
        return [("max", a, j, t, u) for t in range(TT) for u in range(units(a))] + [("negmax", a, j)]

    steps = [("norm", ATT0, 0), ("turn", ATT0, 0), ("keys", 0), ("query", 0, 0),
             ("norm", ATT0, 1), ("turn", ATT0, 1)]
    steps += maxima(0, 0) + [("query", 0, 1)]
    for j in range(J):
        side = {}
        if j + 1 < J:
            spread(side, maxima(0, j + 1), 3 if j else 0, 14)
        if j + 2 < J:
            side.setdefault(1, []).extend([("norm", ATT0, j + 2), ("turn", ATT0, j + 2)])
            side.setdefault(14, []).append(("query", 0, j + 2))
        if j == 0:
            side.setdefault(5, []).append(("keys", 1))
        if j:
            side.setdefault(1, []).append(("mix", 0, j - 1))
            side.setdefault(7, []).append(("norm", FFN0, j - 1))
            side.setdefault(9, []).append(("turn", FFN0, j - 1))
        if j == 2:
            side.setdefault(10, []).append(("route", 0))
            side.setdefault(10, []).append(("zone_load", 0))
            side.setdefault(5, []).append(("wo_split",))
        if j == 3:
            spread(side, [("zone_split", 0, f) for f in range(FC)], 10, 16)
        steps += weave([("attend", 0, j, u) for u in range(HEADS[0] // 2)], side)
    steps += [("attend_end", 0), ("mix", 0, 3), ("heads1",), ("zone_load", 1)]

    side = {}
    per = 2 * FC
    for z in range(Z - 1):
        for f in range(FC):
            side.setdefault(per * z + FC + f + LAG, []).append(("zone_split", z + 1, f))
        if z + 2 < Z:
            side.setdefault(per * z + FC + FC - 1 + LAG, []).append(("zone_load", z + 2))
    side.setdefault(3, []).append(("norm", FFN0, 3))
    side.setdefault(5, []).append(("turn", FFN0, 3))
    side.setdefault(12, []).append(("route", 1))
    for j in range(3):
        end = per * (TOPK * (j // 2) + TOPK - 1) + FC * (j % 2 + 1) - 1
        side.setdefault(end + LAG, []).append(("evac", FFN0, j))
        side.setdefault(end + LAG + 1, []).append(("out", FFN0, j))
    b1 = per * TOPK
    side.setdefault(b1 + 4, []).append(("norm", ATT1, 0))
    side.setdefault(b1 + 6, []).append(("turn", ATT1, 0))
    side.setdefault(b1 + 8, []).append(("query", 1, 0))
    side.setdefault(b1 + 10, []).append(("norm", ATT1, 1))
    side.setdefault(b1 + 13, []).append(("turn", ATT1, 1))
    spread(side, maxima(1, 0), b1 + 14, b1 + 40)
    steps += weave([("zone", s) for s in range(per * Z)], side)
    steps += [("zone_end",), ("evac", FFN0, 3), ("query", 1, 1), ("out", FFN0, 3)]

    for j in range(J):
        side = {}
        if j == 0:
            side.setdefault(0, []).append(("norm", ATT1, 2))
            side.setdefault(2, []).append(("turn", ATT1, 2))
            side.setdefault(3, []).append(("norm", ATT1, 3))
            side.setdefault(5, []).append(("turn", ATT1, 3))
        if j + 1 < J:
            spread(side, maxima(1, j + 1), 3, 7)
        if j + 2 < J:
            side.setdefault(7, []).append(("query", 1, j + 2))
        if j < 3:
            side.setdefault(0, []).append(("ffn_split", j))
        if j:
            side.setdefault(1, []).append(("mix", 1, j - 1))
            side.setdefault(5, []).append(("turn_mix", j - 1))
            side.setdefault(6, []).append(("project", j - 1))
        if j > 1:
            side.setdefault(0, []).append(("norm", FFN1, j - 2))
            side.setdefault(3, []).append(("turn", FFN1, j - 2))
        steps += weave([("attend", 1, j, u) for u in range(HEADS[1] // 2)], side)
    steps += [("attend_end", 1), ("mix", 1, 3), ("norm", FFN1, 2)]
    side = {0: [("turn", FFN1, 2)], 2: [("turn_mix", 3)], 3: [("project", 3)], 4: [("norm", FFN1, 3)],
            6: [("turn", FFN1, 3)]}
    for j in range(J - 1):
        side.setdefault(HC * (j + 1) - 1 + LAG, []).append(("evac", FFN1, j))
        side.setdefault(HC * (j + 1) + LAG, []).append(("out", FFN1, j))
    steps += weave([("gated", s) for s in range(HC * J)], side)
    steps += [("gated_end",), ("evac", FFN1, 3), ("out", FFN1, 3)]
    return steps


def slots_of(step):
    kind = step[0]
    n = {"turn": KC, "query": KC, "max": 1, "negmax": 1, "route": 2, "out": 2, "turn_mix": KC,
         "project": 2, "keys": 5}.get(kind, 0)
    return [step + (i,) for i in range(n)]


def flamingo(nc, x, ctx_t, g_x, g_f, wq0, wk0, wv0, lq1, lq2, lk1, lk2, w1, b1, w2, b2, wa, wb,
             wq1, bq, bq_c, bq_g, wo, bo, wg, wu, wd, ident_in, pick_in, out):
    PLAN = plan()
    order, aux, seen = {}, {}, {}
    for step in PLAN:
        order[step] = seen.get(step[0], 0)
        seen[step[0]] = order[step] + 1
        for key in slots_of(step):
            aux[key] = len(aux)

    ctx = ExitStack()
    with ctx:
        top = [16512]

        def at(name, shape, dt, offset):
            return nc.alloc_sbuf_tensor_at(name, shape, dt, offset=offset)

        def place(name, shape, dt):
            n = 4
            for s in shape[1:]:
                n *= s
            t = at(name, shape, dt, top[0])
            top[0] += -(-n // 32) * 32
            return t

        X = place("X", [P, J * TT, D], F32)
        XN = place("XN", [P, TT, D], F32)
        XH = place("XH", [P, J, KC, NT], F32R)
        XL = place("XL", [P, J, KC, NT], F32R)
        QH = place("QH", [P, KC, NT], F32R)
        QL = place("QL", [P, KC, NT], F32R)
        QG = [place(f"QG{i}", [P, G, NT], F32R) for i in range(2)]
        qg1_at = top[0] - 4 * G * NT
        ka_at = top[0]
        KA0 = place("KA0", [P, B, HEADS[0], S], F32R)
        KA1 = at("KA1", [P, B, HEADS[1], S], F32R, ka_at)
        KA = [KA0, KA1]
        KT1 = place("KT1", [P, G, B * S], F32R)
        V = [place(f"V{a}", [P, B, D // DV, DV + 1], F32) for a in range(2)]
        p_at = top[0]
        PB = [place(f"PB{i}", [P, 2, NT], F32) for i in range(2)]
        o_at = top[0]
        O0 = [place(f"O0{i}", [P, TT, HEADS[0], DV + 1], F32) for i in range(2)]
        wq_at = top[0]
        WQ0H = place("WQ0H", [P, KC, D], F32R)
        WQ0L = place("WQ0L", [P, KC, D], F32R)
        WQ1H = place("WQ1H", [P, KC, D], F32R)
        WQ1L = place("WQ1L", [P, KC, D], F32R)
        NM = place("NM", [P, 2, TT, HEADS[0]], F32)
        NMT = place("NMT", [HEADS[0], NT], F32R)
        ident = place("ident", [P, P], F32)
        pick = place("pick", [P, sum(NS)], F32)
        BOG = place("BOG", [P, D], F32)
        CF = place("CF", [P, HEADS[0]], F32)
        TG = place("TG", [P, 5], F32)
        GIN = place("GIN", [P, 4], F32)
        LAM2 = place("LAM2", [P, 6], F32)
        BQC = place("BQC", [P, KC], F32)
        BQD = place("BQD", [P, G], F32)
        ST = place("ST", [P, TT, 6], F32)
        MV = place("MV", [P, TT, 2], F32)
        RSTD = place("RSTD", [P, 2, TT], F32)
        NHALF = place("NHALF", [P, TT], F32)
        RZ = place("RZ", [P, TT, HEADS[0]], F32)
        POOLED = place("POOLED", [P, KC, J], F32)
        RHID = place("RHID", [RH, 2], F32)
        W1 = place("W1", [P, KC, RH], F32)
        W2 = place("W2", [RH, NZ], F32)
        B1 = place("B1", [RH, 1], F32)
        B2 = place("B2", [P, NZ], F32)
        RT = place("RT", [P, 6, 8], F32)
        RI = place("RI", [P, B, 8], U32)
        WK = place("WK", [P, B, TOPK], F32)
        big = top[0]
        WSA = place("WSA", [P, KC, FF], F32)
        WSB = place("WSB", [P, FC, D], F32)
        split_at = top[0]
        WAH = place("WAH", [P, KC, FF], F32R)
        WAL = place("WAL", [P, KC, FF], F32R)
        WBH = place("WBH", [P, FC, D], F32R)
        WBL = place("WBL", [P, FC, D], F32R)
        assert top[0] <= 229368, top[0]
        top[0] = split_at
        KT0 = place("KT0", [P, G, B * S], F32R)
        WDH = place("WDH", [P, KC, G, 3, 32], F32R)
        WDL = place("WDL", [P, KC, G, 3, 32], F32R)
        WVH = place("WVH", [P, KC, D], F32R)
        WVL = place("WVL", [P, KC, D], F32R)
        CH = place("CH", [P, KC, B * S], F32R)
        CL = place("CL", [P, KC, B * S], F32R)
        CR = place("CR", [P, KC, B * S], F32)
        WOR = place("WOR", [P, KC, D], F32)
        assert top[0] <= 229368, top[0]
        top[0] = big
        WKR = place("WKR", [P, KC, D], F32)
        WVR = place("WVR", [P, KC, D], F32)
        WQR = place("WQR", [P, KC, D], F32)
        WQ1R = place("WQ1R", [P, KC, D], F32)
        BQR = place("BQR", [P, D], F32)
        BOR = place("BOR", [P, D], F32)
        LAM = place("LAM", [P, 4, 8], F32)
        assert top[0] <= split_at
        KT = [KT0, KT1]
        WOH = at("WOH", [P, KC, D], F32R, wq_at)
        WOL = at("WOL", [P, KC, D], F32R, wq_at + 2048)
        HH = [at(f"HH{i}", [P, NT], F32R, p_at + 2048 * i) for i in range(2)]
        HL = [at(f"HL{i}", [P, NT], F32R, p_at + 4096 + 2048 * i) for i in range(2)]
        HF = [at(f"HF{i}", [P, NT], F32, qg1_at + 2048 * i) for i in range(2)]
        SG = [at(f"SG{i}", [P, NT], F32, qg1_at + 4096 + 2048 * i) for i in range(2)]
        O1 = [at(f"O1{i}", [P, TT, HEADS[1], DV + 1], F32, o_at + 4352 * i) for i in range(2)]
        MIX = at("MIX", [P, TT, D], F32, o_at + 8704)
        YS = at("YS", [P, KC, NT], F32, o_at + 8704 + 4096)
        O = [O0, O1]
        top[0] = big
        WI = [place(f"WI{i}", [P, KC * HID], I32) for i in range(2)]
        WGH = place("WGH", [P, KC, HID], F32R)
        WGL = place("WGL", [P, KC, HID], F32R)
        WUH = place("WUH", [P, KC, HID], F32R)
        WUL = place("WUL", [P, KC, HID], F32R)
        WNH = place("WNH", [P, HC, D], F32R)
        WNL = place("WNL", [P, HC, D], F32R)
        assert top[0] <= 229368, top[0]

        SC = ctx.enter_context(nc.psum_tensor("SC", [P, 2, 2, NT], F32))
        PV = ctx.enter_context(nc.psum_tensor("PV", [P, 2, NT], F32))
        AUX = ctx.enter_context(nc.psum_tensor("AUX", [P, 2, NT], F32))

        def sem(name):
            return ctx.enter_context(nc.semaphore(name))

        x_in = [sem(f"x_in{j}") for j in range(J)]
        kv_in, wq0_in, wq1_in, wo_in, small_in = (sem(n) for n in ("kv_in", "wq0_in", "wq1_in", "wo_in", "small_in"))
        zone_in, ffn_in = sem("zone_in"), [sem(f"ffn_in{i}") for i in range(3)]
        q_moved = [sem(f"q_moved{i}") for i in range(2)]
        m_moved = [sem(f"m_moved{i}") for i in range(2)]
        stored = sem("stored")
        aux_ready = sem("aux_ready")
        aux_free = [sem(f"aux_free{i}") for i in range(2)]
        split_hi, split_done = sem("split_hi"), sem("split_done")
        wo_hi, wo_done = sem("wo_hi"), sem("wo_done")
        zsplit_hi, zsplit_done = sem("zsplit_hi"), sem("zsplit_done")
        fsplit_hi, fsplit_done = sem("fsplit_hi"), sem("fsplit_done")
        pool_set, keys_hi, ka_ready = sem("pool_set"), sem("keys_hi"), sem("ka_ready")
        var_ready, rstd_ready, xn_ready = sem("var_ready"), sem("rstd_ready"), sem("xn_ready")
        hi_ready, qh_ready = sem("hi_ready"), sem("qh_ready")
        gates_done, lam_sum, lam_exp, coef_done = (sem(n) for n in ("gates_done", "lam_sum", "lam_exp", "coef_done"))
        sc_ready, exp_done, pv_done, pv_out = (sem(n) for n in ("sc_ready", "exp_done", "pv_done", "pv_out"))
        rz_ready, mixed, mix_hi = sem("rz_ready"), sem("mixed"), sem("mix_hi")
        r_max, r_exp, r_done = sem("r_max"), sem("r_exp"), sem("r_done")
        h_ready, act_done, hl_ready, y_done, ys_ready = (sem(n) for n in ("h_ready", "act_done", "hl_ready", "y_done", "ys_ready"))
        g_ready, silu_done, hf_ready, ghh_ready, ghl_ready, gy_done = (
            sem(n) for n in ("g_ready", "silu_done", "hf_ready", "ghh_ready", "ghl_ready", "gy_done"))
        dve_step, pool_step = sem("dve_step"), sem("pool_step")

        def filled(eng, key):
            eng.wait_ge(aux_ready, aux[key] + 1)

        def used(eng, key):
            eng.wait_ge(aux_free[aux[key] % 2], aux[key] // 2 + 1)

        def bank(key):
            return AUX[:, aux[key] % 2, :]

        def frees(key):
            return aux_free[aux[key] % 2]

        units = [HEADS[a] // 2 for a in range(2)]

        def unit(a, j, u):
            return (J * units[0] if a else 0) + units[a] * j + u

        A0_UNITS, ALL_UNITS = unit(1, 0, 0), unit(1, J, 0)
        PER = 2 * FC
        ZSTEPS, GSTEPS = PER * Z, HC * J
        NORMS = [s for s in PLAN if s[0] == "norm"]
        OUTS = [s for s in PLAN if s[0] == "out"]
        EVACS = [s for s in PLAN if s[0] == "evac"]

        def zone_end_of(j):
            return PER * (TOPK * (j // 2) + TOPK - 1) + FC * (j % 2 + 1)

        block = ctx.enter_context(nc.Block())

        @block.sync
        def _(sp):
            def chunks(ap):
                return ap.rearrange("(c p) n -> p c n", p=P)

            sp.dma_start(X[:, 0:TT, :], x[0]).then_inc(x_in[0], 16)
            for dst, src in ((CR, ctx_t), (WKR, wk0), (WVR, wv0)):
                sp.dma_start(dst[:, :, :], chunks(src)).then_inc(kv_in, 16)
            sp.dma_start(WQR[:, :, :], chunks(wq0)).then_inc(wq0_in, 16)
            for j in range(1, J):
                sp.dma_start(X[:, TT * j:TT * (j + 1), :], x[j]).then_inc(x_in[j], 16)
            sp.dma_start(WQ1R[:, :, :], chunks(wq1)).then_inc(wq1_in, 16)
            sp.dma_start(WOR[:, :, :], chunks(wo)).then_inc(wo_in, 16)
            sp.dma_start(W1[:, :, :], chunks(w1)).then_inc(wo_in, 16)
            for step in PLAN:
                kind = step[0]
                if kind == "query":
                    _, a, j = step
                    n = J * a + j
                    if n >= 2:
                        sp.wait_ge(sc_ready, unit((n - 2) // J, (n - 2) % J, 0) + units[(n - 2) // J])
                    if n == J + 1:
                        sp.wait_ge(hl_ready, ZSTEPS)
                    for c in range(KC):
                        used(sp, step + (c,))
                    for r in range(4):
                        for q, src in enumerate((QH, QL, QH)):
                            dst = QG[n % 2][32 * q:32 * q + 32, :, :].rearrange("p (c r) n -> p c r n", c=KC)[:, :, r, :]
                            sp.dma_start(dst.bitcast(F32), src[32 * r:32 * r + 32, :, :].bitcast(F32)).then_inc(q_moved[n % 2], 16)
                elif kind == "negmax":
                    _, a, j = step
                    n = J * a + j
                    used(sp, step + (0,))
                    for g in range(G):
                        sp.dma_start(QG[n % 2][ROWS:ROWS + NS[a], g, :].bitcast(F32),
                                     NMT[NS[a] * g:NS[a] * (g + 1), :].bitcast(F32)).then_inc(m_moved[n % 2], 16)
                elif kind == "zone_load":
                    z = step[1]
                    sp.wait_ge(r_done, z // TOPK + 1)
                    if z:
                        sp.wait_ge(zsplit_done, FC * z)
                    else:
                        used(sp, ("keys", 1, 4))
                        sp.wait_ge(coef_done, 1)
                    e = sp.value_load(RI[0:1, z // TOPK, z % TOPK:z % TOPK + 1], min_val=0, max_val=NZ - 1)
                    sp.dma_start(WSA[:, :, :], wa[bass.ds(e, 1)].rearrange("a (c p) n -> p (a c) n", p=P)).then_inc(zone_in, 16)
                    sp.dma_start(WSB[:, :, :], wb[bass.ds(e, 1)].rearrange("a (f p) n -> p (a f) n", p=P)).then_inc(zone_in, 16)
                elif kind == "ffn_split":
                    i = step[1]
                    sp.wait_ge(y_done, ZSTEPS)
                    sp.wait_ge(zsplit_done, FC * Z)
                    if i == 2:
                        sp.wait_ge(fsplit_done, 1)
                    dst = WI[i % 2][:, :].rearrange("p (c n) -> p c n", c=HC if i == 2 else KC)
                    sp.dma_start(dst, chunks((wg, wu, wd)[i])).then_inc(ffn_in[i], 16)
                elif kind == "out" and step[1] == FFN1:
                    j = step[2]
                    for i in range(2):
                        used(sp, step + (i,))
                    sp.dma_start(out[j], X[:, TT * j:TT * (j + 1), :]).then_inc(stored, 16)
            sp.wait_ge(stored, 16 * J)

        @block.gpsimd
        def _(pool):
            def spread_row(ap):
                return ap.rearrange("(a n) -> a n", a=1).to_broadcast([P, ap.shape[0]])

            small = [
                (ident[:, :], ident_in), (pick[:, :], pick_in),
                (GIN[:, 0:2], spread_row(g_x)), (GIN[:, 2:4], spread_row(g_f)),
                (LAM[:, 0, :], spread_row(lq1)), (LAM[:, 1, :], spread_row(lq2)),
                (LAM[:, 2, :], spread_row(lk1)), (LAM[:, 3, :], spread_row(lk2)),
                (BOR[:, :], spread_row(bo)), (BQR[:, :], spread_row(bq)), (B2[:, :], spread_row(b2)),
                (W2[:, :], w2), (B1[:, :], b1.rearrange("(p a) -> p a", a=1)),
                (BQC[:, :], bq_c), (BQD[0:ROWS, :], bq_g),
            ]
            assert len(small) == SMALL
            for dst, src in small:
                pool.dma_start(dst, src).then_inc(small_in, 16)
            pool.memset(NHALF[:, :], -0.5).then_inc(pool_set, 1)
            for v in V:
                pool.memset(v[:, :, :, DV:DV + 1], 1.0).then_inc(pool_set, 1)
            pool.wait_ge(pool_set, 3)
            for i, kt in enumerate(KT):
                if i:
                    pool.wait_ge(pool_set, 3 + i)
                pool.memset(kt[ROWS:P, :, :].bitcast(F32), 1.0).then_inc(pool_set, 1)
            pool.wait_ge(pool_set, 5)
            chain = 0
            for step in PLAN:
                kind = step[0]
                if kind == "norm":
                    pool.wait_ge(var_ready, order[step] + 1)
                    pool.tensor_tensor(RSTD[:, 1, :], RSTD[:, 0, :], NHALF[:, :], ALU.pow).then_inc(rstd_ready, 1)
                elif kind == "mix":
                    _, a, j = step
                    n = J * a + j
                    o = O[a][n % 2]
                    xj = X[:, TT * j:TT * (j + 1), :]
                    pool.wait_ge(rz_ready, n + 1)
                    if a == 1:
                        pool.tensor_tensor(xj, xj, BOG[:, :].unsqueeze(1).to_broadcast([P, TT, D]),
                                           ALU.add).then_inc(pool_step, 1)
                        chain += 1
                        if j:
                            filled(pool, ("turn_mix", j - 1, KC - 1))
                    for t in range(TT):
                        rz = RZ[:, t, 0:HEADS[a]].unsqueeze(2).to_broadcast([P, HEADS[a], DV])
                        dst = o[:, t, :, 0:DV] if a == 0 else MIX[:, t, :].rearrange("p (h d) -> p h d", d=DV)
                        if a == 0 or t < TT - 1:
                            pool.tensor_tensor(dst, o[:, t, :, 0:DV], rz, ALU.mult).then_inc(pool_step, 1)
                            chain += 1
                    pool.wait_ge(pool_step, chain)
                    if a == 1:
                        pool.tensor_tensor(dst, o[:, t, :, 0:DV], rz, ALU.mult).then_inc(mixed, 1)
                        continue
                    for half in range(2):
                        for t in range(TT):
                            xh = xj[:, t, :].rearrange("p (h d) -> p h d", d=DV)
                            oh = o[:, t, :, 0:DV].rearrange("p (h two) d -> p h two d", two=2)[:, :, half, :]
                            ins = pool.tensor_tensor(xh, xh, oh, ALU.add)
                            if half == 1 and t == TT - 1:
                                ins.then_inc(mixed, 1)
                            else:
                                ins.then_inc(pool_step, 1)
                                chain += 1
                        if half == 0:
                            pool.wait_ge(pool_step, chain)
                        

        @block.scalar
        def _(act):
            copy, ident_f = ACT.Copy, ACT.Identity

            def dup_hi(raw):
                act.activation(WDH[:, :, :, :, :].rearrange("p c g q r -> p (c g) q r"),
                               raw[:, :, :].rearrange("p c (g r) -> p (c g) r", r=32).unsqueeze(2)
                               .to_broadcast([P, KC * G, 3, 32]), copy).then_inc(split_hi, 1)

            act.wait_ge(kv_in, 48)
            act.activation(CH[:, :, :], CR[:, :, :], copy).then_inc(split_hi, 1)
            dup_hi(WKR)
            act.activation(WVH[:, :, :], WVR[:, :, :], copy).then_inc(split_hi, 1)
            act.wait_ge(wq0_in, 16)
            act.activation(WQ0H[:, :, :], WQR[:, :, :], copy).then_inc(split_hi, 1)

            def attention_out(a, j, u):
                if u % 2 == 0:
                    return
                n, m = unit(a, j, u), J * a + j
                act.wait_ge(pv_done, n + 1)
                if u == 1 and m >= 2:
                    act.wait_ge(mixed, J if m == J else m - 1)
                act.activation(O[a][m % 2][:, :, 2 * u - 2:2 * u + 2, :],
                               PV[:, n // 2 % 2, 0:TT * 4 * (DV + 1)].rearrange("p (t h d) -> p t h d", t=TT, h=4),
                               copy).then_inc(pv_out, 1)

            def gated_hi(s):
                act.wait_ge(hf_ready, s + 1)
                if s >= 2:
                    act.wait_ge(gy_done, s - 1)
                act.activation(HH[s % 2][:, :], HF[s % 2][:, :], copy).then_inc(ghh_ready, 1)

            for step in PLAN:
                kind = step[0]
                if kind == "turn":
                    _, stage, j = step
                    for c in range(KC):
                        filled(act, step + (c,))
                        pooled = {"accum_out": POOLED[:, c, j:j + 1]} if stage == FFN0 else {}
                        act.activation(XH[:, j, c, :], bank(step + (c,)), copy, **pooled).then_inc(hi_ready, 1)
                elif kind == "keys":
                    a = step[1]
                    if a == 1:
                        act.wait_ge(wq1_in, 16)
                        act.activation(WQ1H[:, :, :], WQ1R[:, :, :], copy).then_inc(split_hi, 1)
                        filled(act, ("keys", 0, 4))
                        dup_hi(WQ1R)
                    for i in range(3):
                        key = ("keys", a, i)
                        groups = range(3 * i, min(3 * i + 3, G))
                        filled(act, key)
                        if a == 0:
                            act.activation(KT[0][0:ROWS, groups[0]:groups[-1] + 1, :],
                                           bank(key)[0:ROWS, 0:len(groups) * B * S].rearrange("p (g n) -> p g n", n=B * S),
                                           copy).then_inc(keys_hi, 1)
                            continue
                        for g in groups:
                            at_g = (g - 3 * i) * B * S
                            ins = act.activation(KT[1][0:ROWS, g, :], bank(key)[0:ROWS, at_g:at_g + B * S],
                                                 ident_f, bias=BQD[0:ROWS, g:g + 1])
                        ins.then_inc(keys_hi, 1)
                    if a == 0:
                        act.wait_ge(small_in, 16 * SMALL)
                        act.activation(TG[:, 0:4], GIN[:, :], ACT.Tanh).then_inc(gates_done, 1)
                        act.wait_ge(lam_sum, 1)
                        act.activation(LAM2[:, 2:4], LAM2[:, 0:2], ACT.Exp).then_inc(lam_exp, 1)
                elif kind == "query":
                    _, a, j = step
                    n = J * a + j
                    if n:
                        act.wait_ge(q_moved[(n - 1) % 2], 16 * 12 * ((n - 1) // 2 + 1))
                    for c in range(KC):
                        filled(act, step + (c,))
                        bias = {} if a == 0 else {"bias": BQC[:, c:c + 1]}
                        act.activation(QH[:, c, :], bank(step + (c,)), ident_f if a else copy, **bias).then_inc(qh_ready, 1)
                elif kind == "negmax":
                    _, a, j = step
                    n = J * a + j
                    filled(act, step + (0,))
                    if n:
                        act.wait_ge(m_moved[(n - 1) % 2], 16 * G * ((n - 1) // 2 + 1))
                    act.activation(NMT[0:HEADS[a], :], bank(step + (0,))[0:HEADS[a], :], copy).then_inc(frees(step + (0,)), 1)
                elif kind == "attend":
                    _, a, j, u = step
                    n = unit(a, j, u)
                    act.wait_ge(sc_ready, n + 1)
                    if n >= 2:
                        act.wait_ge(pv_done, n - 1)
                    if a == 1 and n < A0_UNITS + 2:
                        act.wait_ge(y_done, ZSTEPS)
                    act.activation(PB[n % 2][0:S, :, :], SC[0:S, n % 2, :, :], ACT.Exp, scale=SCALE[a]).then_inc(exp_done, 1)
                    if u >= LAG:
                        attention_out(a, j, u - LAG)
                    elif j:
                        attention_out(a, j - 1, units[a] + u - LAG)
                elif kind == "attend_end":
                    a = step[1]
                    for u in range(units[a] - LAG, units[a]):
                        attention_out(a, J - 1, u)
                elif kind == "wo_split":
                    act.wait_ge(wo_in, 32)
                    filled(act, ("query", 0, J - 1, KC - 1))
                    act.activation(WOH[:, :, :], WOR[:, :, :], copy).then_inc(wo_hi, 1)
                elif kind == "route":
                    b = step[1]
                    key = step + (0,)
                    filled(act, key)
                    act.activation(RHID[:, b:b + 1], bank(key)[0:RH, 0:1], ACT.Tanh, bias=B1[:, :],
                                   scale=1.0 / T).then_inc(frees(key), 1)
                    act.wait_ge(r_max, b + 1)
                    act.activation(RT[:, 3, :], RT[:, 0, :], ACT.Exp, bias=RT[:, 2, 0:1],
                                   accum_out=RT[:, 2, 1:2]).then_inc(r_exp, 1)
                elif kind == "zone_split":
                    _, z, f = step
                    act.wait_ge(zone_in, 32 * (z + 1))
                    if z:
                        act.wait_ge(y_done, PER * (z - 1) + FC + f + 1)
                    else:
                        filled(act, ("keys", 1, 4))
                        act.wait_ge(ka_ready, 1)
                        act.wait_ge(wo_done, 1)
                    act.activation(WAH[:, :, P * f:P * (f + 1)], WSA[:, :, P * f:P * (f + 1)], copy).then_inc(zsplit_hi, 1)
                    act.activation(WBH[:, f, :], WSB[:, f, :], copy,
                                   scale=WK[:, z // TOPK, z % TOPK:z % TOPK + 1]).then_inc(zsplit_hi, 1)
                elif kind == "zone":
                    s = step[1]
                    act.wait_ge(h_ready, s + 1)
                    if s >= 2:
                        act.wait_ge(hl_ready, s - 1)
                    else:
                        act.wait_ge(sc_ready, A0_UNITS)
                    act.activation(HF[s % 2][:, :], PV[:, s % 2, :], ACT.Gelu_apprx_tanh)
                    if s >= 2:
                        act.wait_ge(y_done, s - 1)
                    else:
                        act.wait_ge(pv_done, A0_UNITS)
                    act.activation(HH[s % 2][:, :], PV[:, s % 2, :], ACT.Gelu_apprx_tanh).then_inc(act_done, 1)
                elif kind == "evac":
                    _, stage, j = step
                    n = order[step]
                    if n:
                        filled(act, OUTS[n - 1] + (1,))
                    else:
                        act.wait_ge(mixed, J)
                    act.wait_ge(y_done if stage == FFN0 else gy_done, zone_end_of(j) if stage == FFN0 else HC * (j + 1))
                    for c in range(KC):
                        if stage == FFN0:
                            ins = act.activation(YS[:, c, :], SC[:, j % 2, c, :], copy)
                        else:
                            ins = act.activation(YS[:, c, :], PV[:, c, :], copy, scale=TG[:, 4:5])
                    ins.then_inc(ys_ready, 1)
                elif kind == "turn_mix":
                    for c in range(KC):
                        filled(act, step + (c,))
                        act.activation(XH[:, step[1], c, :], bank(step + (c,)), copy).then_inc(mix_hi, 1)
                elif kind == "ffn_split":
                    i = step[1]
                    act.wait_ge(ffn_in[i], 16)
                    src = WI[i % 2][:, :].rearrange("p (c n) -> p c n", c=KC if i < 2 else HC)
                    act.activation((WGH, WUH, WNH)[i][:, :, :], src, copy).then_inc(fsplit_hi, 1)
                elif kind == "gated":
                    s = step[1]
                    act.wait_ge(g_ready, s + 1)
                    if s >= 2:
                        act.wait_ge(hf_ready, s - 1)
                    else:
                        act.wait_ge(sc_ready, ALL_UNITS)
                    act.activation(SG[s % 2][:, :], SC[:, s % 2, 0, :], ACT.Silu, scale=DEQ).then_inc(silu_done, 1)
                    if s:
                        gated_hi(s - 1)
                elif kind == "gated_end":
                    gated_hi(GSTEPS - 1)

        @block.vector
        def _(dve):
            chain = [0]

            def link(ins):
                chain[0] += 1
                ins.then_inc(dve_step, 1)
                dve.wait_ge(dve_step, chain[0])

            def lo_part(dst, raw, hi):
                return dve.tensor_tensor(dst, raw, hi.bitcast(F32), ALU.subtract)

            def dup_lo(raw):
                for c in range(KC):
                    ins = lo_part(WDL[:, c, :, :, :],
                                  raw[:, c, :].rearrange("p (g r) -> p g r", r=32).unsqueeze(2).to_broadcast([P, G, 3, 32]),
                                  WDH[:, c, :, :, :])
                return ins

            def coefficients():
                dve.wait_ge(small_in, 16 * SMALL)
                link(dve.tensor_tensor(LAM[:, 0:2, :], LAM[:, 0:2, :], LAM[:, 2:4, :], ALU.mult))
                dve.tensor_reduce(LAM2[:, 0:2], LAM[:, 0:2, :], AX_X, ALU.add).then_inc(lam_sum, 1)
                link(dve.memset(CF[:, :], 1.0))
                dve.wait_ge(gates_done, 1)
                dve.wait_ge(lam_exp, 1)
                link(dve.scalar_tensor_tensor(LAM2[:, 4:5], LAM2[:, 3:4], LAMBDA_INIT, LAM2[:, 2:3],
                                              ALU.subtract, ALU.subtract))
                cf = CF[:, :].rearrange("p (h two) -> p h two", two=2)
                dve.tensor_scalar(cf[:, :, 0], cf[:, :, 0], TG[:, 0:1], None, ALU.mult)
                dve.tensor_scalar(cf[:, :, 1], cf[:, :, 1], TG[:, 0:1], LAM2[:, 4:5], ALU.mult, ALU.mult)
                dve.tensor_scalar(TG[:, 4:5], TG[:, 3:4], DEQ, None, ALU.mult)
                dve.tensor_scalar(BOG[:, :], BOR[:, :], TG[:, 1:2], None, ALU.mult).then_inc(coef_done, 1)

            def keys_by_head(a):
                rows = ROWS + NS[a]
                for b in range(B):
                    for s in range(NS[a]):
                        dst = KA[a][0:rows, b, :, :].rearrange("p (g s) n -> p g s n", s=NS[a])[:, :, s, :]
                        col = s + (NS[0] if a else 0)
                        ins = dve.tensor_scalar(dst, KT[a][0:rows, :, b * S:(b + 1) * S].bitcast(F32),
                                                pick[0:rows, col:col + 1], None, ALU.mult)
                ins.then_inc(ka_ready, 1)

            dve.wait_ge(split_hi, 1)
            lo_part(CL[:, :, :], CR[:, :, :], CH[:, :, :])
            dve.wait_ge(split_hi, 2)
            dup_lo(WKR)
            dve.wait_ge(split_hi, 3)
            lo_part(WVL[:, :, :], WVR[:, :, :], WVH[:, :, :])
            dve.wait_ge(split_hi, 4)
            lo_part(WQ0L[:, :, :], WQR[:, :, :], WQ0H[:, :, :]).then_inc(split_done, 1)

            for step in PLAN:
                kind = step[0]
                if kind == "norm":
                    _, stage, j = step
                    n = order[step]
                    xj = X[:, TT * j:TT * (j + 1), :]
                    if stage == ATT0:
                        dve.wait_ge(x_in[j], 16)
                    elif stage == FFN0:
                        dve.wait_ge(mixed, j + 1)
                    else:
                        for i in range(2):
                            used(dve, ("out", FFN0, j, i) if stage == ATT1 else ("project", j, i))
                    for t in range(TT):
                        ins = dve.bn_stats(ST[:, t, :], xj[:, t, :])
                    link(ins)
                    for t in range(TT):
                        ins = dve.bn_aggr(MV[:, t, :], ST[:, t, :])
                    link(ins)
                    dve.tensor_scalar(RSTD[:, 0, :], MV[:, :, 1], EPS, None, ALU.add).then_inc(var_ready, 1)
                    dve.wait_ge(rstd_ready, n + 1)
                    if n:
                        filled(dve, ("turn",) + NORMS[n - 1][1:] + (KC - 1,))
                    for t in range(TT):
                        ins = dve.tensor_scalar(XN[:, t, :], xj[:, t, :], MV[:, t, 0:1], RSTD[:, 1, t:t + 1],
                                                ALU.subtract, ALU.mult)
                    ins.then_inc(xn_ready, 1)
                    if stage == FFN0:
                        dve.wait_ge(xn_ready, n + 1)
                        link(dve.scalar_tensor_tensor(xj, XN[:, :, :], TG[:, 2:3], xj, ALU.mult, ALU.add))
                elif kind == "turn":
                    _, stage, j = step
                    for c in range(KC):
                        key = step + (c,)
                        dve.wait_ge(hi_ready, KC * order[step] + c + 1)
                        lo_part(XL[:, j, c, :], bank(key), XH[:, j, c, :]).then_inc(frees(key), 1)
                elif kind == "keys":
                    a = step[1]
                    if a == 1:
                        dve.wait_ge(split_hi, 5)
                        lo_part(WQ1L[:, :, :], WQ1R[:, :, :], WQ1H[:, :, :])
                        dve.wait_ge(split_hi, 6)
                        dup_lo(WQ1R).then_inc(split_done, 1)
                    low = slice(64, ROWS)
                    for i in range(3):
                        key = ("keys", a, i)
                        groups = range(3 * i, min(3 * i + 3, G))
                        dve.wait_ge(keys_hi, 3 * a + i + 1)
                        if a == 0:
                            kt = KT[0][low, groups[0]:groups[-1] + 1, :]
                            ins = lo_part(kt, bank(key)[low, 0:len(groups) * B * S].rearrange("p (g n) -> p g n", n=B * S), kt)
                        else:
                            for g in groups:
                                kt = KT[1][low, g, :]
                                at_g = (g - 3 * i) * B * S
                                ins = dve.scalar_tensor_tensor(kt, bank(key)[low, at_g:at_g + B * S], BQD[low, g:g + 1],
                                                               kt.bitcast(F32), ALU.add, ALU.subtract)
                        ins.then_inc(frees(key), 1)
                    dve.wait_ge(pool_set, 5)
                    dve.wait_ge(small_in, 16 * SMALL)
                    for b in range(B):
                        key = ("keys", a, 3 + b)
                        filled(dve, key)
                        v = V[a][0:S, b, :, 0:DV]
                        ps = bank(key)[0:S, 0:D].rearrange("p (h d) -> p h d", d=DV)
                        if a == 0:
                            ins = dve.tensor_copy(v, ps)
                        else:
                            ins = dve.tensor_tensor(v, ps, BQR[0:S, :].rearrange("p (h d) -> p h d", d=DV), ALU.add)
                        ins.then_inc(frees(key), 1)
                    if a == 0:
                        for i in range(3):
                            used(dve, ("keys", 0, i))
                        keys_by_head(0)
                        coefficients()
                elif kind == "heads1":
                    dve.wait_ge(sc_ready, A0_UNITS)
                    keys_by_head(1)
                elif kind == "query":
                    _, a, j = step
                    for c in range(KC):
                        key = step + (c,)
                        dve.wait_ge(qh_ready, KC * (J * a + j) + c + 1)
                        if a == 0:
                            ins = lo_part(QL[:, c, :], bank(key), QH[:, c, :])
                        else:
                            ins = dve.scalar_tensor_tensor(QL[:, c, :], bank(key), BQC[:, c:c + 1],
                                                           QH[:, c, :].bitcast(F32), ALU.add, ALU.subtract)
                        ins.then_inc(frees(key), 1)
                elif kind == "max":
                    _, a, j, t, u = step
                    n = J * a + j
                    key = step + (0,)
                    if t == 0 and u == 0 and n >= 2:
                        filled(dve, ("negmax", (n - 2) // J, (n - 2) % J, 0))
                    filled(dve, key)
                    dve.tensor_reduce(NM[:, n % 2, t, 4 * u:4 * u + 4], bank(key)[:, 0:4 * S].rearrange("p (h n) -> p h n", h=4),
                                      AX_X, ALU.max, negate=True).then_inc(frees(key), 1)
                elif kind == "mix":
                    _, a, j = step
                    n = J * a + j
                    dve.wait_ge(pv_out, unit(a, j + 1, 0) // 2)
                    if n:
                        dve.wait_ge(mixed, n)
                    rz = RZ[:, :, 0:HEADS[a]]
                    ins = dve.reciprocal(rz, O[a][n % 2][:, :, :, DV])
                    if a == 0:
                        link(ins)
                        ins = dve.tensor_tensor(rz, rz, CF[:, :].unsqueeze(1).to_broadcast([P, TT, HEADS[0]]), ALU.mult)
                    ins.then_inc(rz_ready, 1)
                elif kind == "wo_split":
                    dve.wait_ge(wo_hi, 1)
                    lo_part(WOL[:, :, :], WOR[:, :, :], WOH[:, :, :]).then_inc(wo_done, 1)
                elif kind == "route":
                    b = step[1]
                    key = step + (1,)
                    logits, top_l, aside, ex, top_p, prob = (RT[:, i, :] for i in range(6))
                    filled(dve, key)
                    dve.tensor_tensor(logits, bank(key)[:, 0:NZ], B2[:, :], ALU.add).then_inc(frees(key), 1)
                    used(dve, key)
                    link(dve.max(top_l, logits))
                    dve.tensor_scalar(aside[:, 0:1], top_l[:, 0:1], -1.0, None, ALU.mult).then_inc(r_max, 1)
                    dve.wait_ge(r_exp, b + 1)
                    link(dve.reciprocal(aside[:, 2:3], aside[:, 1:2]))
                    link(dve.tensor_scalar(prob, ex, aside[:, 2:3], None, ALU.mult))
                    link(dve.max(top_p, prob))
                    dve.max_index(RI[:, b, :], top_p, prob)
                    link(dve.tensor_reduce(aside[:, 3:4], top_p[:, 0:TOPK], AX_X, ALU.add))
                    link(dve.reciprocal(aside[:, 4:5], aside[:, 3:4]))
                    dve.tensor_scalar(WK[:, b, :], top_p[:, 0:TOPK], aside[:, 4:5], TG[:, 2:3],
                                      ALU.mult, ALU.mult).then_inc(r_done, 1)
                elif kind == "zone_split":
                    _, z, f = step
                    cols = slice(P * f, P * (f + 1))
                    dve.wait_ge(zsplit_hi, 2 * (FC * z + f) + 1)
                    lo_part(WAL[:, :, cols], WSA[:, :, cols], WAH[:, :, cols])
                    dve.wait_ge(zsplit_hi, 2 * (FC * z + f) + 2)
                    dve.scalar_tensor_tensor(WBL[:, f, :], WSB[:, f, :], WK[:, z // TOPK, z % TOPK:z % TOPK + 1],
                                             WBH[:, f, :].bitcast(F32), ALU.mult, ALU.subtract).then_inc(zsplit_done, 1)
                elif kind == "zone":
                    s = step[1]
                    dve.wait_ge(act_done, s + 1)
                    if s >= 2:
                        dve.wait_ge(y_done, s - 1)
                    else:
                        dve.wait_ge(pv_done, A0_UNITS)
                    lo_part(HL[s % 2][:, :], HF[s % 2][:, :], HH[s % 2][:, :]).then_inc(hl_ready, 1)
                elif kind == "out":
                    _, stage, j = step
                    for i in range(2):
                        key = step + (i,)
                        filled(dve, key)
                        xi = X[:, TT * j + 2 * i:TT * j + 2 * i + 2, :]
                        dve.tensor_tensor(xi, bank(key).rearrange("p (t d) -> p t d", t=2), xi, ALU.add).then_inc(frees(key), 1)
                elif kind == "turn_mix":
                    j = step[1]
                    for c in range(KC):
                        key = step + (c,)
                        dve.wait_ge(mix_hi, KC * j + c + 1)
                        lo_part(XL[:, j, c, :], bank(key), XH[:, j, c, :]).then_inc(frees(key), 1)
                elif kind == "project":
                    j = step[1]
                    for i in range(2):
                        key = step + (i,)
                        filled(dve, key)
                        xi = X[:, TT * j + 2 * i:TT * j + 2 * i + 2, :]
                        dve.scalar_tensor_tensor(xi, bank(key).rearrange("p (t d) -> p t d", t=2), TG[:, 1:2], xi,
                                                 ALU.mult, ALU.add).then_inc(frees(key), 1)
                elif kind == "ffn_split":
                    i = step[1]
                    dve.wait_ge(fsplit_hi, i + 1)
                    src = WI[i % 2][:, :].rearrange("p (c n) -> p c n", c=KC if i < 2 else HC)
                    lo_part((WGL, WUL, WNL)[i][:, :, :], src, (WGH, WUH, WNH)[i][:, :, :]).then_inc(fsplit_done, 1)
                elif kind in ("gated", "gated_end"):
                    s = step[1] if kind == "gated" else GSTEPS
                    if kind == "gated":
                        dve.wait_ge(silu_done, s + 1)
                        if s >= 2:
                            dve.wait_ge(ghl_ready, s - 1)
                        dve.scalar_tensor_tensor(HF[s % 2][:, :], SC[:, s % 2, 1, :], DEQ, SG[s % 2][:, :],
                                                 ALU.mult, ALU.mult).then_inc(hf_ready, 1)
                    if s:
                        dve.wait_ge(ghh_ready, s)
                        if s >= 3:
                            dve.wait_ge(gy_done, s - 2)
                        lo_part(HL[(s - 1) % 2][:, :], HF[(s - 1) % 2][:, :], HH[(s - 1) % 2][:, :]).then_inc(ghl_ready, 1)

        @block.tensor
        def _(pe):
            def fill(key):
                n = aux[key]
                if n >= 2:
                    pe.wait_ge(aux_free[n % 2], n // 2)
                return AUX[:, n % 2, :]

            def product(ps, terms, start=True, stop=True):
                passes = [p for lh, ll, rh, rl in terms for p in ((lh, rh), (lh, rl), (ll, rh))]
                for i, (lhs, rhs) in enumerate(passes):
                    ins = pe.matmul(ps, lhs, rhs, start=start and i == 0, stop=stop and i == len(passes) - 1)
                return ins

            def attend_values(m):
                a = 1 if m >= A0_UNITS else 0
                j, u = divmod(m - (A0_UNITS if a else 0), units[a])
                pe.wait_ge(exp_done, m + 1)
                quad = m // 2
                if u % 2 == 0 and quad >= 2:
                    pe.wait_ge(pv_out, quad - 1)
                ps = PV[:, quad % 2, 0:TT * 4 * (DV + 1)].rearrange("p (t h d) -> p t h d", t=TT, h=4)
                for i in range(2):
                    h = 2 * u + i
                    for t in range(TT):
                        ins = pe.matmul(ps[:, t, h % 4, :], PB[m % 2][0:S, i, P * t:P * (t + 1)],
                                        V[a][0:S, j // 2, h // 2 if a == 0 else h, :], start=True, stop=True)
                ins.then_inc(pv_done, 1)

            def zone_out(s):
                z, nt, f = s // PER, s % PER // FC, s % FC
                pe.wait_ge(hl_ready, s + 1)
                first, last = z % TOPK == 0 and f == 0, z % TOPK == TOPK - 1 and f == FC - 1
                if first and z:
                    pe.wait_ge(ys_ready, nt + 1)
                for c in range(KC):
                    cols = slice(P * c, P * (c + 1))
                    ins = product(SC[:, nt, c, :], [(WBH[:, f, cols], WBL[:, f, cols], HH[s % 2][:, :], HL[s % 2][:, :])],
                                  start=first, stop=last)
                ins.then_inc(y_done, 1)

            def gated_out(s):
                j, f = divmod(s, HC)
                pe.wait_ge(ghl_ready, s + 1)
                if f == 0:
                    if j:
                        pe.wait_ge(ys_ready, J + j)
                    else:
                        pe.wait_ge(fsplit_done, 3)
                        pe.wait_ge(pv_out, ALL_UNITS // 2)
                for c in range(KC):
                    cols = slice(P * c, P * (c + 1))
                    ins = product(PV[:, c, :], [(WNH[:, f, cols], WNL[:, f, cols], HH[s % 2][:, :], HL[s % 2][:, :])],
                                  start=f == 0, stop=f == HC - 1)
                ins.then_inc(gy_done, 1)

            pe.wait_ge(small_in, 16 * SMALL)
            for step in PLAN:
                kind = step[0]
                if kind == "turn":
                    pe.wait_ge(xn_ready, order[step] + 1)
                    for c in range(KC):
                        ps = fill(step + (c,))
                        for t in range(TT):
                            ins = pe.transpose(ps[:, P * t:P * (t + 1)], XN[:, t, P * c:P * (c + 1)], ident[:, :])
                        ins.then_inc(aux_ready, 1)
                elif kind == "keys":
                    a = step[1]
                    pe.wait_ge(split_done, a + 1)
                    for i in range(3):
                        ps = fill(step + (i,))
                        for g in range(3 * i, min(3 * i + 3, G)):
                            terms = [(WDH[:, c, g, :, :].rearrange("p q r -> p (q r)"), WDL[:, c, g, :, :].rearrange("p q r -> p (q r)"),
                                      CH[:, c, :], CL[:, c, :]) for c in range(KC)]
                            ins = product(ps[0:ROWS, (g - 3 * i) * B * S:(g - 3 * i + 1) * B * S], terms)
                        ins.then_inc(aux_ready, 1)
                    vh, vl = (WVH, WVL) if a == 0 else (WQ1H, WQ1L)
                    for b in range(B):
                        ps = fill(step + (3 + b,))
                        cols = slice(b * S, (b + 1) * S)
                        product(ps[0:S, 0:D], [(CH[:, c, cols], CL[:, c, cols], vh[:, c, :], vl[:, c, :])
                                               for c in range(KC)]).then_inc(aux_ready, 1)
                elif kind == "query":
                    _, a, j = step
                    for c in range(KC):
                        used(pe, ("turn", ATT1 if a else ATT0, j, c))
                    wh, wl = (WQ1H, WQ1L) if a else (WQ0H, WQ0L)
                    if a == 0:
                        pe.wait_ge(split_done, 1)
                    for c in range(KC):
                        cols = slice(P * c, P * (c + 1))
                        product(fill(step + (c,)), [(wh[:, k, cols], wl[:, k, cols], XH[:, j, k, :], XL[:, j, k, :])
                                                    for k in range(KC)]).then_inc(aux_ready, 1)
                elif kind == "max":
                    _, a, j, t, u = step
                    n = J * a + j
                    if t == 0 and u == 0:
                        pe.wait_ge(q_moved[n % 2], 16 * 12 * (n // 2 + 1))
                        pe.wait_ge(ka_ready, a + 1)
                    ps = fill(step + (0,))
                    for i in range(4 // NS[a]):
                        g = u * (4 // NS[a]) + i
                        n_cols = NS[a] * S
                        ins = pe.matmul(ps[:, i * n_cols:(i + 1) * n_cols], QG[n % 2][0:ROWS, g, P * t:P * (t + 1)],
                                        KA[a][0:ROWS, j // 2, NS[a] * g:NS[a] * (g + 1), :].rearrange("p h n -> p (h n)"),
                                        start=True, stop=True)
                    ins.then_inc(aux_ready, 1)
                elif kind == "negmax":
                    _, a, j = step
                    last = 8 if a == 0 else 4
                    for u in (last - 2, last - 1):
                        used(pe, ("max", a, j, TT - 1, u, 0))
                    ps = fill(step + (0,))
                    for t in range(TT):
                        ins = pe.transpose(ps[0:HEADS[a], P * t:P * (t + 1)], NM[:, (J * a + j) % 2, t, 0:HEADS[a]], ident[:, :])
                    ins.then_inc(aux_ready, 1)
                elif kind == "attend":
                    _, a, j, u = step
                    n, m = unit(a, j, u), J * a + j
                    if u == 0:
                        pe.wait_ge(m_moved[m % 2], 16 * G * (m // 2 + 1))
                    if a == 1 and n < A0_UNITS + 2:
                        pe.wait_ge(ys_ready, 3 + n - A0_UNITS)
                    if n >= 2:
                        pe.wait_ge(exp_done, n - 1)
                    rows = ROWS + NS[a]
                    for i in range(2):
                        h = 2 * u + i
                        ins = pe.matmul(SC[0:S, n % 2, i, :], KA[a][0:rows, j // 2, h, :], QG[m % 2][0:rows, h // NS[a], :],
                                        start=True, stop=True)
                    ins.then_inc(sc_ready, 1)
                    if n - unit(a, 0, 0) >= LAG:
                        attend_values(n - LAG)
                elif kind == "attend_end":
                    for m in range(unit(step[1] + 1, 0, 0) - LAG if step[1] == 0 else ALL_UNITS - LAG,
                                   A0_UNITS if step[1] == 0 else ALL_UNITS):
                        attend_values(m)
                elif kind == "route":
                    b = step[1]
                    pe.wait_ge(wo_in, 32)
                    key = step + (0,)
                    ps = fill(key)
                    cols = [(c, 2 * b + i) for c in range(KC) for i in range(2)]
                    for c in range(KC):
                        used(pe, ("turn", FFN0, 2 * b + 1, c))
                    for i, (c, j) in enumerate(cols):
                        ins = pe.matmul(ps[0:RH, 0:1], W1[:, c, :], POOLED[:, c, j:j + 1], start=i == 0, stop=i == len(cols) - 1)
                    ins.then_inc(aux_ready, 1)
                    used(pe, key)
                    pe.matmul(fill(step + (1,))[:, 0:NZ], RHID[:, b:b + 1].to_broadcast([RH, P]), W2[:, :],
                              start=True, stop=True).then_inc(aux_ready, 1)
                elif kind == "zone":
                    s = step[1]
                    z, nt, f = s // PER, s % PER // FC, s % FC
                    j = 2 * (z // TOPK) + nt
                    if z % TOPK == 0 and f == 0:
                        for c in range(KC):
                            used(pe, ("turn", FFN0, j, c))
                    if nt == 0:
                        pe.wait_ge(zsplit_done, FC * z + f + 1)
                    if s >= 2:
                        pe.wait_ge(act_done, s - 1)
                    else:
                        pe.wait_ge(pv_out, A0_UNITS // 2)
                    cols = slice(P * f, P * (f + 1))
                    product(PV[:, s % 2, :], [(WAH[:, c, cols], WAL[:, c, cols], XH[:, j, c, :], XL[:, j, c, :])
                                              for c in range(KC)]).then_inc(h_ready, 1)
                    if s >= LAG:
                        zone_out(s - LAG)
                elif kind == "zone_end":
                    for s in range(ZSTEPS - LAG, ZSTEPS):
                        zone_out(s)
                elif kind == "out":
                    pe.wait_ge(ys_ready, order[step] + 1)
                    for i in range(2):
                        ps = fill(step + (i,))
                        for t in (2 * i, 2 * i + 1):
                            for c in range(KC):
                                at_c = D * (t % 2) + P * c
                                ins = pe.transpose(ps[:, at_c:at_c + P], YS[:, c, P * t:P * (t + 1)], ident[:, :])
                        ins.then_inc(aux_ready, 1)
                elif kind == "turn_mix":
                    j = step[1]
                    pe.wait_ge(mixed, J + j + 1)
                    for c in range(KC):
                        ps = fill(step + (c,))
                        for t in range(TT):
                            ins = pe.transpose(ps[:, P * t:P * (t + 1)], MIX[:, t, P * c:P * (c + 1)], ident[:, :])
                        ins.then_inc(aux_ready, 1)
                elif kind == "project":
                    j = step[1]
                    pe.wait_ge(wo_done, 1)
                    for c in range(KC):
                        used(pe, ("turn_mix", j, c))
                    for i in range(2):
                        ps = fill(step + (i,))
                        for t in (2 * i, 2 * i + 1):
                            rows = slice(P * t, P * (t + 1))
                            ins = product(ps[:, D * (t % 2):D * (t % 2 + 1)],
                                          [(XH[:, j, k, rows], XL[:, j, k, rows], WOH[:, k, :], WOL[:, k, :]) for k in range(KC)])
                        ins.then_inc(aux_ready, 1)
                elif kind == "gated":
                    s = step[1]
                    j, f = divmod(s, HC)
                    if f == 0:
                        pe.wait_ge(fsplit_done, 2)
                        for c in range(KC):
                            used(pe, ("turn", FFN1, j, c))
                    if s >= 2:
                        pe.wait_ge(hf_ready, s - 1)
                    else:
                        pe.wait_ge(exp_done, ALL_UNITS)
                    cols = slice(P * f, P * (f + 1))
                    for i, (wh, wl) in enumerate(((WGH, WGL), (WUH, WUL))):
                        ins = product(SC[:, s % 2, i, :], [(wh[:, c, cols], wl[:, c, cols], XH[:, j, c, :], XL[:, j, c, :])
                                                           for c in range(KC)])
                    ins.then_inc(g_ready, 1)
                    if s >= LAG:
                        gated_out(s - LAG)
                elif kind == "gated_end":
                    for s in range(GSTEPS - LAG, GSTEPS):
                        gated_out(s)


def kernel(**inputs):
    import numpy as np
    import concourse.bacc as bacc
    from concourse.bass_utils import run_bass_kernel_spmd as run

    x = np.asarray(inputs["x"])
    shape = x.shape
    tiles = x.reshape(J, TT, P, D).transpose(0, 2, 1, 3)
    pick = np.zeros((P, sum(NS)), np.float32)
    for a in range(2):
        for s in range(NS[a]):
            size = 32 // NS[a]
            for q in range(3):
                pick[32 * q + size * s:32 * q + size * (s + 1), s + a * NS[0]] = 1.0
            pick[ROWS + s, s + a * NS[0]] = 1.0
    bq = np.asarray(inputs["L1_xattn_bq"])
    arrays = {
        "x": tiles,
        "ctx_t": np.asarray(inputs["ctx_1024"]).reshape(B * S, D).T,
        "g_x": inputs["g_xattn"], "g_f": inputs["g_ffn"],
        "wq0": np.asarray(inputs["L0_xattn_Wq"]).T, "wk0": np.asarray(inputs["L0_xattn_Wk"]).T,
        "wv0": np.asarray(inputs["L0_xattn_Wv"]).T,
        "lq1": inputs["L0_xattn_lambda_q1"], "lq2": inputs["L0_xattn_lambda_q2"],
        "lk1": inputs["L0_xattn_lambda_k1"], "lk2": inputs["L0_xattn_lambda_k2"],
        "w1": inputs["L0_ffn_W1"], "b1": inputs["L0_ffn_b1"], "w2": inputs["L0_ffn_W2"], "b2": inputs["L0_ffn_b2"],
        "wa": inputs["L0_ffn_Wa"], "wb": inputs["L0_ffn_Wb"],
        "wq1": inputs["L1_xattn_Wq"], "bq": bq,
        "bq_c": bq.reshape(KC, P).T, "bq_g": np.tile(bq.reshape(G, 32).T, (3, 1)),
        "wo": inputs["L1_xattn_Wo"], "bo": inputs["L1_xattn_bo"],
        "wg": np.asarray(inputs["L1_ffn_w_gate"]).T, "wu": np.asarray(inputs["L1_ffn_w_up"]).T,
        "wd": np.asarray(inputs["L1_ffn_w_down"]).T,
        "ident": np.eye(P, dtype=np.float32), "pick": pick,
    }
    nc = bacc.Bacc("TRN2", target_bir_lowering=False, num_devices=1)
    fed, args = {}, []
    for name, a in arrays.items():
        a = np.ascontiguousarray(a)
        fed[f"in_{name}"] = a
        args.append(nc.dram_tensor(f"in_{name}", a.shape, mybir.dt.from_np(a.dtype), kind="ExternalInput").ap())
    args.append(nc.dram_tensor("out_x", tiles.shape, F32, kind="ExternalOutput").ap())
    flamingo(nc, *args)
    r = run(nc, [fed], core_ids=[0])
    got = np.asarray(r.results[0]["out_x"])
    return got.transpose(0, 2, 1, 3).reshape(shape)
```

```python
from contextlib import ExitStack

import concourse.bass as bass
from concourse import mybir

F32 = mybir.dt.float32
F32R = mybir.dt.float32r
I32 = mybir.dt.int32
U32 = mybir.dt.uint32
ALU = mybir.AluOpType
ACT = mybir.ActivationFunctionType
AX_X = mybir.AxisListType.X

P = 128
B, T, D, S = 2, 1024, 256, 77
NT = 512
J = B * T // NT
TT = NT // P
KC = D // P
G = D // 32
HEADS = (32, 16)
NS = tuple(h // G for h in HEADS)
DV = 16
SCALE = (8 ** -0.5, 16 ** -0.5)
LAMBDA_INIT = 0.8
EPS = 1e-5
NZ, TOPK, RH, FF = 8, 3, 64, 1024
FC = FF // P
Z = B * TOPK
HID = 768
HC = HID // P
DEQ = 1.0 / 127.0
ATT0, FFN0, ATT1, FFN1 = range(4)
SMALL = 13
SCALE_LAG = 3
LAG = 2
ROWS = 96


def weave(main, side):
    out = []
    for n, step in enumerate(main):
        out.append(step)
        out += side.get(n, [])
    return out


def spread(side, steps, first, last):
    for i, s in enumerate(steps):
        side.setdefault(first + i * (last - first) // len(steps), []).append(s)


def attention_tile(a, j, side, filler, first, last):
    out, gaps = [], []
    for u in range(HEADS[a] // 2):
        out.append(("attend", a, j, u))
        if first <= u < last:
            gaps.append(len(out))
        if u % 2 == 0:
            out.append(("quad_turn", a, j, u))
            if first <= u < last:
                gaps.append(len(out))
            out.append(("quad_values", a, j, u))
        out += side.get(u, [])
    at = {}
    if filler:
        for i, step in enumerate(filler):
            at.setdefault(gaps[i * len(gaps) // len(filler)], []).append(step)
    whole = list(at.get(0, []))
    for i, step in enumerate(out):
        whole.append(step)
        whole += at.get(i + 1, [])
    return whole


def plan():
    def units(a):
        return 8 if a == 0 else 4

    def maxima(a, j):
        half = units(a) // 2
        return [("max", a, j, t, c * half + u) for c in range(KC) for t in range(TT)
                for u in range(half)] + [("negmax", a, j)]

    def moves(a, j):
        return [("q_move", a, j, c) for c in range(KC)]

    steps = [("norm", ATT0, 0), ("weights_split", 0), ("turn", ATT0, 0), ("weights_split", 1),
             ("query", 0, 0)] + moves(0, 0)
    steps += [("keys", 0)]
    steps += weave(maxima(0, 0), {3: [("norm", ATT0, 1)], 9: [("turn", ATT0, 1)],
                                  13: [("query", 0, 1)] + moves(0, 1), 26: [("weights_split", 2)]})
    steps += [("coefficients",), ("keys", 1)]
    for j in range(J):
        side = {}
        filler = maxima(0, j + 1) if j + 1 < J else []
        if j + 2 < J:
            side.setdefault(1, []).append(("norm", ATT0, j + 2))
            side.setdefault(3, []).append(("turn", ATT0, j + 2))
            side.setdefault(6, []).append(("query", 0, j + 2))
            side.setdefault(7, []).append(("q_move", 0, j + 2, 0))
            side.setdefault(15, []).append(("q_move", 0, j + 2, 1))
        if j:
            side.setdefault(4, []).append(("mix", 0, j - 1))
            side.setdefault(11, []).append(("norm", FFN0, j - 1))
            side.setdefault(13, []).append(("turn", FFN0, j - 1))
            side.setdefault(15, []).append(("residual", j - 1))
        if j == 2:
            side.setdefault(14, []).extend([("route", 0), ("zone_load", 0)])
            side.setdefault(5, []).append(("wo_split",))
        if j == 3:
            spread(side, [("zone_split", 0, f) for f in range(FC // 2)], 10, 16)
        steps += attention_tile(0, j, side, filler, 0, 12)
    steps += [("attend_end", 0), ("zone_load2", 0), ("mix", 0, 3), ("heads1",), ("zone_load", 1), ("zone_load2", 1)]

    side = {}
    per = 2 * FC
    for z in range(Z - 1):
        for f in range(FC):
            side.setdefault(per * z + FC + f + LAG, []).append(("zone_split", z + 1, f))
        if z + 2 < Z:
            side.setdefault(per * z + FC + FC - 1 + LAG, []).extend([("zone_load", z + 2), ("zone_load2", z + 2)])
    for f in range(FC // 2, FC):
        side.setdefault(f - FC // 2, []).append(("zone_split", 0, f))
    side.setdefault(3, []).append(("norm", FFN0, 3))
    side.setdefault(5, []).append(("turn", FFN0, 3))
    side.setdefault(7, []).append(("residual", 3))
    side.setdefault(12, []).append(("route", 1))
    for j in range(3):
        end = per * (TOPK * (j // 2) + TOPK - 1) + FC * (j % 2 + 1) - 1
        side.setdefault(end + LAG, []).append(("evac", FFN0, j))
        side.setdefault(end + LAG + 1, []).append(("out", FFN0, j))
    b1 = per * TOPK
    side.setdefault(b1 + 4, []).append(("norm", ATT1, 0))
    side.setdefault(b1 + 6, []).append(("turn", ATT1, 0))
    side.setdefault(b1 + 8, []).extend([("query", 1, 0)] + moves(1, 0))
    side.setdefault(b1 + 10, []).append(("norm", ATT1, 1))
    side.setdefault(b1 + 13, []).append(("turn", ATT1, 1))
    side.setdefault(b1 + 16, []).extend([("query", 1, 1)] + moves(1, 1))
    spread(side, maxima(1, 0), b1 + 14, b1 + 27)
    spread(side, maxima(1, 1), b1 + 27, b1 + 43)
    side.setdefault(b1 + 44, []).append(("norm", ATT1, 2))
    side.setdefault(b1 + 46, []).append(("turn", ATT1, 2))
    steps += weave([("zone", s) for s in range(per * Z)], side)
    steps += [("zone_end",), ("evac", FFN0, 3), ("query", 1, 2), ("out", FFN0, 3)]

    for j in range(J):
        side = {}
        if j == 0:
            side.setdefault(0, []).append(("norm", ATT1, 3))
            side.setdefault(5, []).extend([("ffn_load", 0), ("ffn_load", 1)])
            side.setdefault(3, []).append(("turn", ATT1, 3))
            side.setdefault(3, []).append(("q_move", 1, 2, 0))
            side.setdefault(7, []).append(("q_move", 1, 2, 1))
        if j == 1:
            side.setdefault(4, []).append(("query", 1, 3))
            side.setdefault(1, []).append(("ffn_split", 0))
            side.setdefault(2, []).append(("ffn_load", 2))
            side.setdefault(6, []).append(("ffn_split", 1))
            side.setdefault(5, []).append(("q_move", 1, 3, 0))
            side.setdefault(7, []).append(("q_move", 1, 3, 1))
        if j == 2:
            side.setdefault(6, []).append(("ffn_split", 2))
        filler = maxima(1, j + 1) if 0 < j < J - 1 else []
        if j:
            side.setdefault(3, []).append(("mix", 1, j - 1))
            side.setdefault(7, []).extend([("turn_mix", j - 1), ("project", j - 1)])
        if j > 1:
            side.setdefault(0, []).append(("norm", FFN1, j - 2))
            side.setdefault(3, []).append(("turn", FFN1, j - 2))
        steps += attention_tile(1, j, side, filler, 1, 8)
    steps += [("attend_end", 1), ("mix", 1, 3), ("norm", FFN1, 2)]
    side = {1: [("turn", FFN1, 2)], 3: [("turn_mix", 3)], 5: [("project", 3)], 6: [("norm", FFN1, 3)],
            10: [("turn", FFN1, 3)]}
    for j in range(J - 1):
        side.setdefault(HC * (j + 1) - 1 + LAG, []).append(("evac", FFN1, j))
        side.setdefault(HC * (j + 1) + LAG, []).append(("out", FFN1, j))
    steps += weave([("gated", s) for s in range(HC * J)], side)
    steps += [("gated_end",), ("evac", FFN1, 3), ("out", FFN1, 3)]
    placed, waiting = [], []
    for step in steps:
        if waiting and (step == ("turn",) + waiting[0][1:] or waiting[1] == 0):
            placed.append(waiting[0])
            waiting = []
        placed.append(step)
        if step[0] == "norm":
            waiting = [("scale",) + step[1:], SCALE_LAG]
        elif waiting:
            waiting[1] -= 1
    return placed


def slots_of(step):
    kind = step[0]
    n = {"turn": KC, "query": KC, "max": 1, "negmax": 1, "route": 2, "out": 2, "turn_mix": KC,
         "project": 2, "keys": 5}.get(kind, 0)
    return [step + (i,) for i in range(n)]


def flamingo(nc, x, ctx_t, g_x, g_f, wq0, wk0, wv0, lq1, lq2, lk1, lk2, w1, b1, w2, b2, wa, wb,
             wq1, bq, bq_c, bq_g, wo, bo, wg, wu, wd, ident_in, pick_in, out):
    PLAN = plan()
    order, aux, seen = {}, {}, {}
    for step in PLAN:
        order[step] = seen.get(step[0], 0)
        seen[step[0]] = order[step] + 1
        for key in slots_of(step):
            aux[key] = len(aux)

    ctx = ExitStack()
    with ctx:
        top = [16512]

        def at(name, shape, dt, offset):
            return nc.alloc_sbuf_tensor_at(name, shape, dt, offset=offset)

        def place(name, shape, dt):
            n = 4
            for s in shape[1:]:
                n *= s
            t = at(name, shape, dt, top[0])
            top[0] += -(-n // 32) * 32
            return t

        X = place("X", [P, J * TT, D], F32)
        XN = place("XN", [P, TT, D], F32)
        XH = place("XH", [P, J, KC, NT], F32R)
        XL = place("XL", [P, J, KC, NT], F32R)
        QH = place("QH", [P, KC, NT], F32R)
        QL = place("QL", [P, KC, NT], F32R)
        QG = [place(f"QG{i}", [P, G, NT], F32R) for i in range(2)]
        qg1_at = top[0] - 4 * G * NT
        ka_at = top[0]
        KA0 = place("KA0", [P, B, HEADS[0], S], F32R)
        KA1 = at("KA1", [P, B, HEADS[1], S], F32R, ka_at)
        KA = [KA0, KA1]
        KT1 = place("KT1", [P, G, B * S], F32R)
        V = [place(f"V{a}", [P, B, D // DV, DV + 1], F32) for a in range(2)]
        p_at = top[0]
        PB = [place(f"PB{i}", [P, 2, NT], F32) for i in range(2)]
        o_at = top[0]
        O0 = [place(f"O0{i}", [P, TT, HEADS[0], DV + 1], F32) for i in range(2)]
        wq_at = top[0]
        WQ0H = place("WQ0H", [P, KC, D], F32R)
        WQ0L = place("WQ0L", [P, KC, D], F32R)
        WQ1H = place("WQ1H", [P, KC, D], F32R)
        WQ1L = place("WQ1L", [P, KC, D], F32R)
        NM = place("NM", [P, 2, TT, HEADS[0]], F32)
        NMT = place("NMT", [HEADS[0], NT], F32R)
        ident = place("ident", [P, P], F32)
        pick = place("pick", [P, sum(NS)], F32)
        BOG = place("BOG", [P, D], F32)
        CF = place("CF", [P, HEADS[0]], F32)
        TG = place("TG", [P, 5], F32)
        GIN = place("GIN", [P, 4], F32)
        LAM2 = place("LAM2", [P, 6], F32)
        BQC = place("BQC", [P, KC], F32)
        BQD = place("BQD", [P, G], F32)
        ST = place("ST", [P, TT, 6], F32)
        MV = place("MV", [P, TT, 2], F32)
        RSTD = place("RSTD", [P, 2, TT], F32)
        NHALF = place("NHALF", [P, TT], F32)
        RZ = place("RZ", [P, TT, HEADS[0]], F32)
        POOLED = place("POOLED", [P, KC, J], F32)
        RHID = place("RHID", [RH, 2], F32)
        W1 = place("W1", [P, KC, RH], F32)
        W2 = place("W2", [RH, NZ], F32)
        B1 = place("B1", [RH, 1], F32)
        B2 = place("B2", [P, NZ], F32)
        RT = place("RT", [P, 6, 8], F32)
        RI = place("RI", [P, B, 8], U32)
        WK = place("WK", [P, B, TOPK], F32)
        big = top[0]
        WSA = place("WSA", [P, KC, FF], F32)
        WSB = place("WSB", [P, FC, D], F32)
        split_at = top[0]
        WAH = place("WAH", [P, KC, FF], F32R)
        WAL = place("WAL", [P, KC, FF], F32R)
        WBH = place("WBH", [P, FC, D], F32R)
        WBL = place("WBL", [P, FC, D], F32R)
        assert top[0] <= 229368, top[0]
        vt_at = top[0] - 4 * KC * NT
        VT0 = at("VT0", [P, KC, NT], F32, vt_at)
        top[0] = split_at
        KT0 = place("KT0", [P, G, B * S], F32R)
        WDH = place("WDH", [P, KC, G, 3, 32], F32R)
        WDL = place("WDL", [P, KC, G, 3, 32], F32R)
        WVH = place("WVH", [P, KC, D], F32R)
        WVL = place("WVL", [P, KC, D], F32R)
        CH = place("CH", [P, KC, B * S], F32R)
        CL = place("CL", [P, KC, B * S], F32R)
        CR = place("CR", [P, KC, B * S], F32)
        WOR = place("WOR", [P, KC, D], F32)
        assert top[0] <= vt_at, top[0]
        top[0] = big
        WKR = place("WKR", [P, KC, D], F32)
        WVR = place("WVR", [P, KC, D], F32)
        WQR = place("WQR", [P, KC, D], F32)
        WQ1R = place("WQ1R", [P, KC, D], F32)
        BQR = place("BQR", [P, D], F32)
        BOR = place("BOR", [P, D], F32)
        LAM = place("LAM", [P, 4, 8], F32)
        pb_at = split_at - 8 * NT
        assert top[0] <= pb_at
        KT = [KT0, KT1]
        PB2 = [at("PB20", [P, 2, NT], F32, pb_at),
               at("PB21", [P, 2, NT], F32, ka_at + 4 * B * HEADS[1] * S)]
        WOH = at("WOH", [P, KC, D], F32R, wq_at)
        WOL = at("WOL", [P, KC, D], F32R, wq_at + 2048)
        HH = [at(f"HH{i}", [P, NT], F32R, p_at + 2048 * i) for i in range(2)]
        HL = [at(f"HL{i}", [P, NT], F32R, p_at + 4096 + 2048 * i) for i in range(2)]
        HF = [at(f"HF{i}", [P, NT], F32, ka_at + 4 * B * HEADS[1] * S + 2048 * i) for i in range(2)]
        SG = [at(f"SG{i}", [P, NT], F32, qg1_at + 2048 * i) for i in range(2)]
        O1 = [at(f"O1{i}", [P, TT, HEADS[1], DV + 1], F32, o_at + 4352 * i) for i in range(2)]
        MIX = at("MIX", [P, TT, D], F32, o_at + 8704)
        YS = at("YS", [P, KC, NT], F32, o_at + 8704 + 4096)
        O = [O0, O1]
        VT = [VT0, YS]
        top[0] = big
        WI = [place(f"WI{i}", [P, KC * HID], I32) for i in range(2)]
        WGH = place("WGH", [P, KC, HID], F32R)
        WGL = place("WGL", [P, KC, HID], F32R)
        WUH = place("WUH", [P, KC, HID], F32R)
        WUL = place("WUL", [P, KC, HID], F32R)
        WNH = place("WNH", [P, HC, D], F32R)
        WNL = place("WNL", [P, HC, D], F32R)
        assert top[0] <= 229368, top[0]

        SC = ctx.enter_context(nc.psum_tensor("SC", [P, 2, 2, NT], F32))
        PV = ctx.enter_context(nc.psum_tensor("PV", [P, 2, NT], F32))
        AUX = ctx.enter_context(nc.psum_tensor("AUX", [P, 2, NT], F32))

        def sem(name):
            return ctx.enter_context(nc.semaphore(name))

        x_in = [sem(f"x_in{j}") for j in range(J)]
        kv_in, wq0_in, wq1_in, wo_in, small_in = (sem(n) for n in ("kv_in", "wq0_in", "wq1_in", "wo_in", "small_in"))
        const_in, late_in = sem("const_in"), sem("late_in")
        zone_in, ffn_in = sem("zone_in"), [sem(f"ffn_in{i}") for i in range(3)]
        q_moved = [[sem(f"q_moved{i}{c}") for c in range(KC)] for i in range(2)]
        m_moved = [sem(f"m_moved{i}") for i in range(2)]
        stored = sem("stored")
        aux_ready = sem("aux_ready")
        aux_free = [sem(f"aux_free{i}") for i in range(2)]
        split_hi, split_done = sem("split_hi"), sem("split_done")
        wo_hi, wo_done = sem("wo_hi"), sem("wo_done")
        zsplit_hi, zsplit_done = sem("zsplit_hi"), sem("zsplit_done")
        fsplit_hi, fsplit_done = sem("fsplit_hi"), sem("fsplit_done")
        pool_set, keys_hi, ka_ready = sem("pool_set"), sem("keys_hi"), sem("ka_ready")
        var_ready, rstd_ready, xn_ready = sem("var_ready"), sem("rstd_ready"), sem("xn_ready")
        hi_ready, qh_ready = sem("hi_ready"), sem("qh_ready")
        gates_done, lam_sum, lam_exp, coef_done = (sem(n) for n in ("gates_done", "lam_sum", "lam_exp", "coef_done"))
        sc_ready, exp_done, pv_done, pv_out = (sem(n) for n in ("sc_ready", "exp_done", "pv_done", "pv_out"))
        pv_set, vt_ready, vt_turned = sem("pv_set"), sem("vt_ready"), sem("vt_turned")
        rz_ready, mixed, mix_hi = sem("rz_ready"), sem("mixed"), sem("mix_hi")
        r_max, r_exp, r_done = sem("r_max"), sem("r_exp"), sem("r_done")
        h_ready, act_done, hl_ready, y_done, ys_ready = (sem(n) for n in ("h_ready", "act_done", "hl_ready", "y_done", "ys_ready"))
        g_ready, silu_done, hf_ready, ghh_ready, ghl_ready, gy_done = (
            sem(n) for n in ("g_ready", "silu_done", "hf_ready", "ghh_ready", "ghl_ready", "gy_done"))
        dve_step, pool_step = sem("dve_step"), sem("pool_step")
        added = sem("added")

        def filled(eng, key):
            eng.wait_ge(aux_ready, aux[key] + 1)

        def used(eng, key):
            eng.wait_ge(aux_free[aux[key] % 2], aux[key] // 2 + 1)

        def bank(key):
            return AUX[:, aux[key] % 2, :]

        def frees(key):
            return aux_free[aux[key] % 2]

        units = [HEADS[a] // 2 for a in range(2)]

        def unit(a, j, u):
            return (J * units[0] if a else 0) + units[a] * j + u

        def probs(n):
            return PB[n % 3] if n % 3 < 2 else PB2[0 if n < A0_UNITS else 1]

        A0_UNITS, ALL_UNITS = unit(1, 0, 0), unit(1, J, 0)
        PER = 2 * FC
        ZSTEPS, GSTEPS = PER * Z, HC * J
        NORMS = [s for s in PLAN if s[0] == "norm"]
        OUTS = [s for s in PLAN if s[0] == "out"]
        EVACS = [s for s in PLAN if s[0] == "evac"]

        def zone_end_of(j):
            return PER * (TOPK * (j // 2) + TOPK - 1) + FC * (j % 2 + 1)

        block = ctx.enter_context(nc.Block())

        @block.sync
        def _(sp):
            def chunks(ap):
                return ap.rearrange("(c p) n -> p c n", p=P)

            sp.dma_start(X[:, 0:TT, :], x[0]).then_inc(x_in[0], 16)
            sp.dma_start(WQR[:, :, :], chunks(wq0)).then_inc(wq0_in, 16)
            for dst, src in ((CR, ctx_t), (WKR, wk0), (WVR, wv0)):
                sp.dma_start(dst[:, :, :], chunks(src)).then_inc(kv_in, 16)
            for j in range(1, J):
                sp.dma_start(X[:, TT * j:TT * (j + 1), :], x[j]).then_inc(x_in[j], 16)
            sp.dma_start(WQ1R[:, :, :], chunks(wq1)).then_inc(wq1_in, 16)
            sp.dma_start(WOR[:, :, :], chunks(wo)).then_inc(wo_in, 16)
            sp.dma_start(W1[:, :, :], chunks(w1)).then_inc(wo_in, 16)
            for step in PLAN:
                kind = step[0]
                if kind == "q_move":
                    _, a, j, c = step
                    n = J * a + j
                    if n >= 2:
                        sp.wait_ge(sc_ready, unit((n - 2) // J, (n - 2) % J, 0) + units[(n - 2) // J] * (c + 1) // KC)
                    used(sp, ("query", a, j, c))
                    for r in range(4):
                        for q, src in enumerate((QH, QL, QH)):
                            sp.dma_start(QG[n % 2][32 * q:32 * q + 32, 4 * c + r, :].bitcast(F32),
                                         src[32 * r:32 * r + 32, c, :].bitcast(F32)).then_inc(q_moved[n % 2][c], 16)
                elif kind == "negmax":
                    _, a, j = step
                    n = J * a + j
                    used(sp, step + (0,))
                    for g in range(G):
                        sp.dma_start(QG[n % 2][ROWS:ROWS + NS[a], g, :].bitcast(F32),
                                     NMT[NS[a] * g:NS[a] * (g + 1), :].bitcast(F32)).then_inc(m_moved[n % 2], 16)
                elif kind == "zone_load":
                    z = step[1]
                    sp.wait_ge(r_done, z // TOPK + 1)
                    if z:
                        sp.wait_ge(zsplit_done, FC * z)
                    else:
                        used(sp, ("keys", 1, 4))
                        sp.wait_ge(coef_done, 1)
                    e = sp.value_load(RI[0:1, z // TOPK, z % TOPK:z % TOPK + 1], min_val=0, max_val=NZ - 1)
                    sp.dma_start(WSA[:, :, :], wa[bass.ds(e, 1)].rearrange("a (c p) n -> p (a c) n", p=P)).then_inc(zone_in, 16)
                    second = wb[bass.ds(e, 1)].rearrange("a (f p) n -> p (a f) n", p=P)
                    sp.dma_start(WSB[:, 0:FC // 2, :], second[:, 0:FC // 2, :]).then_inc(zone_in, 16)
                elif kind == "zone_load2":
                    z = step[1]
                    if z == 0:
                        sp.wait_ge(pv_done, A0_UNITS // 2)
                    second = wb[bass.ds(e, 1)].rearrange("a (f p) n -> p (a f) n", p=P)
                    sp.dma_start(WSB[:, FC // 2:FC, :], second[:, FC // 2:FC, :]).then_inc(late_in, 16)
                elif kind == "ffn_load":
                    i = step[1]
                    sp.wait_ge(y_done, ZSTEPS)
                    sp.wait_ge(zsplit_done, FC * Z)
                    if i == 2:
                        sp.wait_ge(fsplit_done, 1)
                    dst = WI[i % 2][:, :].rearrange("p (c n) -> p c n", c=HC if i == 2 else KC)
                    sp.dma_start(dst, chunks((wg, wu, wd)[i])).then_inc(ffn_in[i], 16)
                elif kind == "out" and step[1] == FFN1:
                    j = step[2]
                    for i in range(2):
                        used(sp, step + (i,))
                    sp.dma_start(out[j], X[:, TT * j:TT * (j + 1), :]).then_inc(stored, 16)
            sp.wait_ge(stored, 16 * J)

        @block.gpsimd
        def _(pool):
            def spread_row(ap):
                return ap.rearrange("(a n) -> a n", a=1).to_broadcast([P, ap.shape[0]])

            small = [
                (GIN[:, 0:2], spread_row(g_x)), (GIN[:, 2:4], spread_row(g_f)),
                (LAM[:, 0, :], spread_row(lq1)), (LAM[:, 1, :], spread_row(lq2)),
                (LAM[:, 2, :], spread_row(lk1)), (LAM[:, 3, :], spread_row(lk2)),
                (BOR[:, :], spread_row(bo)), (BQR[:, :], spread_row(bq)), (B2[:, :], spread_row(b2)),
                (W2[:, :], w2), (B1[:, :], b1.rearrange("(p a) -> p a", a=1)),
                (BQC[:, :], bq_c), (BQD[0:ROWS, :], bq_g),
            ]
            assert len(small) == SMALL
            pool.memset(NHALF[:, :], -0.5).then_inc(pool_set, 1)
            for v in V:
                pool.memset(v[:, :, :, DV:DV + 1], 1.0).then_inc(pool_set, 1)
            pool.wait_ge(pool_set, 3)
            for i, kt in enumerate(KT):
                if i:
                    pool.wait_ge(pool_set, 3 + i)
                pool.memset(kt[ROWS:P, :, :].bitcast(F32), 1.0).then_inc(pool_set, 1)
            pool.wait_ge(pool_set, 5)
            chain = 0
            for step in PLAN:
                kind = step[0]
                if kind == "norm":
                    pool.wait_ge(var_ready, order[step] + 1)
                    pool.tensor_tensor(RSTD[:, 1, :], RSTD[:, 0, :], NHALF[:, :], ALU.pow).then_inc(rstd_ready, 1)
                elif kind == "weights_split" and step[1] == 0:
                    for dst, src in small:
                        pool.dma_start(dst, src).then_inc(small_in, 16)
                elif kind == "mix":
                    _, a, j = step
                    n = J * a + j
                    o = O[a][n % 2]
                    xj = X[:, TT * j:TT * (j + 1), :]
                    pool.wait_ge(rz_ready, n + 1)
                    if a == 1:
                        pool.tensor_tensor(xj, xj, BOG[:, :].unsqueeze(1).to_broadcast([P, TT, D]),
                                           ALU.add).then_inc(pool_step, 1)
                        chain += 1
                        if j:
                            filled(pool, ("turn_mix", j - 1, KC - 1))
                    for t in range(TT):
                        rz = RZ[:, t, 0:HEADS[a]].unsqueeze(2).to_broadcast([P, HEADS[a], DV])
                        dst = o[:, t, :, 0:DV] if a == 0 else MIX[:, t, :].rearrange("p (h d) -> p h d", d=DV)
                        if a == 0 or t < TT - 1:
                            pool.tensor_tensor(dst, o[:, t, :, 0:DV], rz, ALU.mult).then_inc(pool_step, 1)
                            chain += 1
                    pool.wait_ge(pool_step, chain)
                    if a == 1:
                        pool.tensor_tensor(dst, o[:, t, :, 0:DV], rz, ALU.mult).then_inc(mixed, 1)
                        continue
                    for half in range(2):
                        for t in range(TT):
                            xh = xj[:, t, :].rearrange("p (h d) -> p h d", d=DV)
                            oh = o[:, t, :, 0:DV].rearrange("p (h two) d -> p h two d", two=2)[:, :, half, :]
                            ins = pool.tensor_tensor(xh, xh, oh, ALU.add)
                            if half == 1 and t == TT - 1:
                                ins.then_inc(mixed, 1)
                            else:
                                ins.then_inc(pool_step, 1)
                                chain += 1
                        if half == 0:
                            pool.wait_ge(pool_step, chain)


        @block.scalar
        def _(act):
            copy, ident_f = ACT.Copy, ACT.Identity

            def dup_hi(raw):
                act.activation(WDH[:, :, :, :, :].rearrange("p c g q r -> p (c g) q r"),
                               raw[:, :, :].rearrange("p c (g r) -> p (c g) r", r=32).unsqueeze(2)
                               .to_broadcast([P, KC * G, 3, 32]), copy).then_inc(split_hi, 1)

            for dst, src in ((ident, ident_in), (pick, pick_in)):
                act.dma_start(dst[:, :], src).then_inc(const_in, 16)

            def values_out(n):
                if n % 2 == 0 or n < 3:
                    return
                q = (n - 3) // 2
                act.wait_ge(pv_done, q + 1)
                if q >= 2:
                    act.wait_ge(vt_turned, q - 1)
                act.activation(VT[1 if q >= A0_UNITS // 2 else 0][:, q % 2, :], PV[:, q % 2, :], copy).then_inc(vt_ready, 1)

            def gated_hi(s):
                act.wait_ge(hf_ready, s + 1)
                if s >= 2:
                    act.wait_ge(gy_done, s - 1)
                act.activation(HH[s % 2][:, :], HF[s % 2][:, :], copy).then_inc(ghh_ready, 1)

            for step in PLAN:
                kind = step[0]
                if kind == "weights_split" and step[1] == 0:
                    act.wait_ge(wq0_in, 16)
                    act.activation(WQ0H[:, :, :], WQR[:, :, :], copy).then_inc(split_hi, 1)
                elif kind == "weights_split" and step[1] == 2:
                    act.wait_ge(wq1_in, 16)
                    act.activation(WQ1H[:, :, :], WQ1R[:, :, :], copy).then_inc(split_hi, 1)
                    filled(act, ("keys", 0, 4))
                    dup_hi(WQ1R)
                elif kind == "weights_split":
                    act.wait_ge(kv_in, 48)
                    act.activation(CH[:, :, :], CR[:, :, :], copy).then_inc(split_hi, 1)
                    dup_hi(WKR)
                    act.activation(WVH[:, :, :], WVR[:, :, :], copy).then_inc(split_hi, 1)
                elif kind == "turn":
                    _, stage, j = step
                    for c in range(KC):
                        filled(act, step + (c,))
                        pooled = {"accum_out": POOLED[:, c, j:j + 1]} if stage == FFN0 else {}
                        act.activation(XH[:, j, c, :], bank(step + (c,)), copy, **pooled).then_inc(hi_ready, 1)
                elif kind == "keys":
                    a = step[1]
                    for i in range(3):
                        key = ("keys", a, i)
                        groups = range(3 * i, min(3 * i + 3, G))
                        filled(act, key)
                        if a == 0:
                            act.activation(KT[0][0:ROWS, groups[0]:groups[-1] + 1, :],
                                           bank(key)[0:ROWS, 0:len(groups) * B * S].rearrange("p (g n) -> p g n", n=B * S),
                                           copy).then_inc(keys_hi, 1)
                            continue
                        for g in groups:
                            at_g = (g - 3 * i) * B * S
                            ins = act.activation(KT[1][0:ROWS, g, :], bank(key)[0:ROWS, at_g:at_g + B * S],
                                                 ident_f, bias=BQD[0:ROWS, g:g + 1])
                        ins.then_inc(keys_hi, 1)
                elif kind == "coefficients":
                    act.wait_ge(small_in, 16 * SMALL)
                    act.activation(TG[:, 0:4], GIN[:, :], ACT.Tanh).then_inc(gates_done, 1)
                    act.wait_ge(lam_sum, 1)
                    act.activation(LAM2[:, 2:4], LAM2[:, 0:2], ACT.Exp).then_inc(lam_exp, 1)
                elif kind == "query":
                    _, a, j = step
                    n = J * a + j
                    if n:
                        for c in range(KC):
                            act.wait_ge(q_moved[(n - 1) % 2][c], 16 * 12 * ((n - 1) // 2 + 1))
                    for c in range(KC):
                        filled(act, step + (c,))
                        bias = {} if a == 0 else {"bias": BQC[:, c:c + 1]}
                        act.activation(QH[:, c, :], bank(step + (c,)), ident_f if a else copy, **bias).then_inc(qh_ready, 1)
                elif kind == "negmax":
                    _, a, j = step
                    n = J * a + j
                    filled(act, step + (0,))
                    if n:
                        act.wait_ge(m_moved[(n - 1) % 2], 16 * G * ((n - 1) // 2 + 1))
                    act.activation(NMT[0:HEADS[a], :], bank(step + (0,))[0:HEADS[a], :], copy).then_inc(frees(step + (0,)), 1)
                elif kind == "attend":
                    _, a, j, u = step
                    n = unit(a, j, u)
                    if n == A0_UNITS:
                        filled(act, ("out", FFN0, J - 1, 1))
                    if n != A0_UNITS + 1:
                        values_out(n)
                    act.wait_ge(sc_ready, n + 1)
                    if n >= 3:
                        act.wait_ge(pv_done, (n - 3) // 2 + 1)
                    if a == 1 and n < A0_UNITS + 3:
                        act.wait_ge(y_done, ZSTEPS)
                    act.activation(probs(n)[0:S, :, :], SC[0:S, n % 2, :, :], ACT.Exp, scale=SCALE[a]).then_inc(exp_done, 1)
                elif kind == "attend_end":
                    values_out((ALL_UNITS if step[1] else A0_UNITS) + 1)
                elif kind == "wo_split":
                    act.wait_ge(wo_in, 32)
                    filled(act, ("query", 0, J - 1, KC - 1))
                    act.activation(WOH[:, :, :], WOR[:, :, :], copy).then_inc(wo_hi, 1)
                elif kind == "route":
                    b = step[1]
                    key = step + (0,)
                    filled(act, key)
                    act.activation(RHID[:, b:b + 1], bank(key)[0:RH, 0:1], ACT.Tanh, bias=B1[:, :],
                                   scale=1.0 / T).then_inc(frees(key), 1)
                    act.wait_ge(r_max, b + 1)
                    act.activation(RT[:, 3, :], RT[:, 0, :], ACT.Exp, bias=RT[:, 2, 0:1],
                                   accum_out=RT[:, 2, 1:2]).then_inc(r_exp, 1)
                elif kind == "zone_split":
                    _, z, f = step
                    act.wait_ge(zone_in, 32 * (z + 1))
                    if f >= FC // 2:
                        act.wait_ge(late_in, 16 * (z + 1))
                    if z:
                        act.wait_ge(y_done, PER * (z - 1) + FC + f + 1)
                    else:
                        filled(act, ("keys", 1, 4))
                        act.wait_ge(ka_ready, 1)
                        act.wait_ge(wo_done, 1)
                    act.activation(WAH[:, :, P * f:P * (f + 1)], WSA[:, :, P * f:P * (f + 1)], copy).then_inc(zsplit_hi, 1)
                    act.activation(WBH[:, f, :], WSB[:, f, :], copy,
                                   scale=WK[:, z // TOPK, z % TOPK:z % TOPK + 1]).then_inc(zsplit_hi, 1)
                elif kind == "zone":
                    s = step[1]
                    act.wait_ge(h_ready, s + 1)
                    if s >= 2:
                        act.wait_ge(hl_ready, s - 1)
                    else:
                        act.wait_ge(sc_ready, A0_UNITS)
                    act.activation(HF[s % 2][:, :], PV[:, s % 2, :], ACT.Gelu_apprx_tanh)
                    if s >= 2:
                        act.wait_ge(y_done, s - 1)
                    else:
                        act.wait_ge(pv_done, A0_UNITS // 2)
                    act.activation(HH[s % 2][:, :], PV[:, s % 2, :], ACT.Gelu_apprx_tanh).then_inc(act_done, 1)
                elif kind == "evac":
                    _, stage, j = step
                    n = order[step]
                    if n == J:
                        act.wait_ge(vt_turned, ALL_UNITS // 2)
                    elif n:
                        filled(act, OUTS[n - 1] + (1,))
                    else:
                        act.wait_ge(mixed, J)
                    act.wait_ge(y_done if stage == FFN0 else gy_done, zone_end_of(j) if stage == FFN0 else HC * (j + 1))
                    for c in range(KC):
                        if stage == FFN0:
                            ins = act.activation(YS[:, c, :], SC[:, j % 2, c, :], copy)
                        else:
                            ins = act.activation(YS[:, c, :], PV[:, c, :], copy, scale=TG[:, 4:5])
                    ins.then_inc(ys_ready, 1)
                elif kind == "turn_mix":
                    for c in range(KC):
                        filled(act, step + (c,))
                        act.activation(XH[:, step[1], c, :], bank(step + (c,)), copy).then_inc(mix_hi, 1)
                elif kind == "ffn_split":
                    i = step[1]
                    act.wait_ge(ffn_in[i], 16)
                    src = WI[i % 2][:, :].rearrange("p (c n) -> p c n", c=KC if i < 2 else HC)
                    act.activation((WGH, WUH, WNH)[i][:, :, :], src, copy).then_inc(fsplit_hi, 1)
                elif kind == "gated":
                    s = step[1]
                    act.wait_ge(g_ready, s + 1)
                    if s >= 2:
                        act.wait_ge(hf_ready, s - 1)
                    else:
                        act.wait_ge(sc_ready, ALL_UNITS)
                    act.activation(SG[s % 2][:, :], SC[:, s % 2, 0, :], ACT.Silu, scale=DEQ).then_inc(silu_done, 1)
                    if s:
                        gated_hi(s - 1)
                elif kind == "gated_end":
                    gated_hi(GSTEPS - 1)

        @block.vector
        def _(dve):
            chain = [0]
            dve.memset(PV[:, :, :], 0.0).then_inc(pv_set, 1)

            def link(ins):
                chain[0] += 1
                ins.then_inc(dve_step, 1)
                dve.wait_ge(dve_step, chain[0])

            def lo_part(dst, raw, hi):
                return dve.tensor_tensor(dst, raw, hi.bitcast(F32), ALU.subtract)

            def dup_lo(raw):
                for c in range(KC):
                    ins = lo_part(WDL[:, c, :, :, :],
                                  raw[:, c, :].rearrange("p (g r) -> p g r", r=32).unsqueeze(2).to_broadcast([P, G, 3, 32]),
                                  WDH[:, c, :, :, :])
                return ins

            def outputs_out(q):
                a = 1 if q >= A0_UNITS // 2 else 0
                j, u = divmod(2 * q - (A0_UNITS if a else 0), units[a])
                m = J * a + j
                dve.wait_ge(vt_turned, q + 1)
                if u == 0 and m >= 2:
                    dve.wait_ge(mixed, J if m == J else m - 1)
                dve.tensor_copy(O[a][m % 2][:, :, 2 * u:2 * u + 4, :],
                                PV[:, q % 2, :].rearrange("p (t h d) -> p t h d", t=TT, d=32)[:, :, :, 0:DV + 1]
                                ).then_inc(pv_out, 1)

            def coefficients():
                dve.wait_ge(small_in, 16 * SMALL)
                link(dve.tensor_tensor(LAM[:, 0:2, :], LAM[:, 0:2, :], LAM[:, 2:4, :], ALU.mult))
                dve.tensor_reduce(LAM2[:, 0:2], LAM[:, 0:2, :], AX_X, ALU.add).then_inc(lam_sum, 1)
                link(dve.memset(CF[:, :], 1.0))
                dve.wait_ge(gates_done, 1)
                dve.wait_ge(lam_exp, 1)
                link(dve.scalar_tensor_tensor(LAM2[:, 4:5], LAM2[:, 3:4], LAMBDA_INIT, LAM2[:, 2:3],
                                              ALU.subtract, ALU.subtract))
                cf = CF[:, :].rearrange("p (h two) -> p h two", two=2)
                dve.tensor_scalar(cf[:, :, 0], cf[:, :, 0], TG[:, 0:1], None, ALU.mult)
                dve.tensor_scalar(cf[:, :, 1], cf[:, :, 1], TG[:, 0:1], LAM2[:, 4:5], ALU.mult, ALU.mult)
                dve.tensor_scalar(TG[:, 4:5], TG[:, 3:4], DEQ, None, ALU.mult)
                dve.tensor_scalar(BOG[:, :], BOR[:, :], TG[:, 1:2], None, ALU.mult).then_inc(coef_done, 1)

            def keys_by_head(a):
                rows = ROWS + NS[a]
                for b in range(B):
                    for s in range(NS[a]):
                        dst = KA[a][0:rows, b, :, :].rearrange("p (g s) n -> p g s n", s=NS[a])[:, :, s, :]
                        col = s + (NS[0] if a else 0)
                        ins = dve.tensor_scalar(dst, KT[a][0:rows, :, b * S:(b + 1) * S].bitcast(F32),
                                                pick[0:rows, col:col + 1], None, ALU.mult)
                ins.then_inc(ka_ready, 1)

            for step in PLAN:
                kind = step[0]
                if kind == "weights_split" and step[1] == 0:
                    dve.wait_ge(split_hi, 1)
                    lo_part(WQ0L[:, :, :], WQR[:, :, :], WQ0H[:, :, :]).then_inc(split_done, 1)
                elif kind == "weights_split" and step[1] == 2:
                    dve.wait_ge(split_hi, 5)
                    lo_part(WQ1L[:, :, :], WQ1R[:, :, :], WQ1H[:, :, :])
                    dve.wait_ge(split_hi, 6)
                    dup_lo(WQ1R).then_inc(split_done, 1)
                elif kind == "weights_split":
                    dve.wait_ge(split_hi, 2)
                    lo_part(CL[:, :, :], CR[:, :, :], CH[:, :, :])
                    dve.wait_ge(split_hi, 3)
                    dup_lo(WKR)
                    dve.wait_ge(split_hi, 4)
                    lo_part(WVL[:, :, :], WVR[:, :, :], WVH[:, :, :]).then_inc(split_done, 1)
                elif kind == "norm":
                    _, stage, j = step
                    n = order[step]
                    xj = X[:, TT * j:TT * (j + 1), :]
                    if stage == ATT0:
                        dve.wait_ge(x_in[j], 16)
                    elif stage == FFN0:
                        dve.wait_ge(mixed, j + 1)
                    else:
                        for i in range(2):
                            used(dve, ("out", FFN0, j, i) if stage == ATT1 else ("project", j, i))
                    if n:
                        dve.wait_ge(xn_ready, n)
                    for t in range(TT):
                        ins = dve.bn_stats(ST[:, t, :], xj[:, t, :])
                    link(ins)
                    for t in range(TT):
                        ins = dve.bn_aggr(MV[:, t, :], ST[:, t, :])
                    link(ins)
                    dve.tensor_scalar(RSTD[:, 0, :], MV[:, :, 1], EPS, None, ALU.add).then_inc(var_ready, 1)
                elif kind == "scale":
                    _, stage, j = step
                    n = order[step]
                    dve.wait_ge(rstd_ready, n + 1)
                    if n:
                        filled(dve, ("turn",) + NORMS[n - 1][1:] + (KC - 1,))
                        if NORMS[n - 1][1] == FFN0:
                            dve.wait_ge(added, NORMS[n - 1][2] + 1)
                    for t in range(TT):
                        ins = dve.tensor_scalar(XN[:, t, :], X[:, TT * j + t, :], MV[:, t, 0:1], RSTD[:, 1, t:t + 1],
                                                ALU.subtract, ALU.mult)
                    ins.then_inc(xn_ready, 1)
                elif kind == "residual":
                    j = step[1]
                    dve.wait_ge(xn_ready, order["norm", FFN0, j] + 1)
                    xj = X[:, TT * j:TT * (j + 1), :]
                    dve.scalar_tensor_tensor(xj, XN[:, :, :], TG[:, 2:3], xj, ALU.mult, ALU.add).then_inc(added, 1)
                elif kind == "turn":
                    _, stage, j = step
                    for c in range(KC):
                        key = step + (c,)
                        dve.wait_ge(hi_ready, KC * order[step] + c + 1)
                        lo_part(XL[:, j, c, :], bank(key), XH[:, j, c, :]).then_inc(frees(key), 1)
                elif kind == "keys":
                    a = step[1]
                    low = slice(64, ROWS)
                    for i in range(3):
                        key = ("keys", a, i)
                        groups = range(3 * i, min(3 * i + 3, G))
                        dve.wait_ge(keys_hi, 3 * a + i + 1)
                        if a == 0:
                            kt = KT[0][low, groups[0]:groups[-1] + 1, :]
                            ins = lo_part(kt, bank(key)[low, 0:len(groups) * B * S].rearrange("p (g n) -> p g n", n=B * S), kt)
                        else:
                            for g in groups:
                                kt = KT[1][low, g, :]
                                at_g = (g - 3 * i) * B * S
                                ins = dve.scalar_tensor_tensor(kt, bank(key)[low, at_g:at_g + B * S], BQD[low, g:g + 1],
                                                               kt.bitcast(F32), ALU.add, ALU.subtract)
                        ins.then_inc(frees(key), 1)
                    dve.wait_ge(pool_set, 5)
                    dve.wait_ge(const_in, 32)
                    if a == 1:
                        dve.wait_ge(small_in, 16 * SMALL)
                    for b in range(B):
                        key = ("keys", a, 3 + b)
                        filled(dve, key)
                        v = V[a][0:S, b, :, 0:DV]
                        ps = bank(key)[0:S, 0:D].rearrange("p (h d) -> p h d", d=DV)
                        if a == 0:
                            ins = dve.tensor_copy(v, ps)
                        else:
                            ins = dve.tensor_tensor(v, ps, BQR[0:S, :].rearrange("p (h d) -> p h d", d=DV), ALU.add)
                        ins.then_inc(frees(key), 1)
                    if a == 0:
                        for i in range(3):
                            used(dve, ("keys", 0, i))
                        keys_by_head(0)
                elif kind == "coefficients":
                    coefficients()
                elif kind == "heads1":
                    dve.wait_ge(sc_ready, A0_UNITS)
                    keys_by_head(1)
                elif kind == "query":
                    _, a, j = step
                    for c in range(KC):
                        key = step + (c,)
                        dve.wait_ge(qh_ready, KC * (J * a + j) + c + 1)
                        if a == 0:
                            ins = lo_part(QL[:, c, :], bank(key), QH[:, c, :])
                        else:
                            ins = dve.scalar_tensor_tensor(QL[:, c, :], bank(key), BQC[:, c:c + 1],
                                                           QH[:, c, :].bitcast(F32), ALU.add, ALU.subtract)
                        ins.then_inc(frees(key), 1)
                elif kind == "max":
                    _, a, j, t, u = step
                    n = J * a + j
                    key = step + (0,)
                    if t == 0 and u == 0 and n >= 2:
                        filled(dve, ("negmax", (n - 2) // J, (n - 2) % J, 0))
                    filled(dve, key)
                    dve.tensor_reduce(NM[:, n % 2, t, 4 * u:4 * u + 4], bank(key)[:, 0:4 * S].rearrange("p (h n) -> p h n", h=4),
                                      AX_X, ALU.max, negate=True).then_inc(frees(key), 1)
                elif kind == "attend":
                    _, a, j, u = step
                    n = unit(a, j, u)
                    if n % 2 and n - 5 >= unit(a, 0, 0):
                        outputs_out((n - 5) // 2)
                elif kind == "attend_end":
                    end = (ALL_UNITS if step[1] else A0_UNITS) // 2
                    for q in (end - 2, end - 1):
                        outputs_out(q)
                elif kind == "mix":
                    _, a, j = step
                    n = J * a + j
                    dve.wait_ge(pv_out, unit(a, j + 1, 0) // 2)
                    if n:
                        dve.wait_ge(mixed, n)
                    rz = RZ[:, :, 0:HEADS[a]]
                    ins = dve.reciprocal(rz, O[a][n % 2][:, :, :, DV])
                    if a == 0:
                        link(ins)
                        ins = dve.tensor_tensor(rz, rz, CF[:, :].unsqueeze(1).to_broadcast([P, TT, HEADS[0]]), ALU.mult)
                    ins.then_inc(rz_ready, 1)
                elif kind == "wo_split":
                    dve.wait_ge(wo_hi, 1)
                    lo_part(WOL[:, :, :], WOR[:, :, :], WOH[:, :, :]).then_inc(wo_done, 1)
                elif kind == "route":
                    b = step[1]
                    key = step + (1,)
                    logits, top_l, aside, ex, top_p, prob = (RT[:, i, :] for i in range(6))
                    filled(dve, key)
                    dve.tensor_tensor(logits, bank(key)[:, 0:NZ], B2[:, :], ALU.add).then_inc(frees(key), 1)
                    used(dve, key)
                    link(dve.max(top_l, logits))
                    dve.tensor_scalar(aside[:, 0:1], top_l[:, 0:1], -1.0, None, ALU.mult).then_inc(r_max, 1)
                    dve.wait_ge(r_exp, b + 1)
                    link(dve.reciprocal(aside[:, 2:3], aside[:, 1:2]))
                    link(dve.tensor_scalar(prob, ex, aside[:, 2:3], None, ALU.mult))
                    link(dve.max(top_p, prob))
                    dve.max_index(RI[:, b, :], top_p, prob)
                    link(dve.tensor_reduce(aside[:, 3:4], top_p[:, 0:TOPK], AX_X, ALU.add))
                    link(dve.reciprocal(aside[:, 4:5], aside[:, 3:4]))
                    dve.tensor_scalar(WK[:, b, :], top_p[:, 0:TOPK], aside[:, 4:5], TG[:, 2:3],
                                      ALU.mult, ALU.mult).then_inc(r_done, 1)
                elif kind == "zone_split":
                    _, z, f = step
                    cols = slice(P * f, P * (f + 1))
                    dve.wait_ge(zsplit_hi, 2 * (FC * z + f) + 1)
                    lo_part(WAL[:, :, cols], WSA[:, :, cols], WAH[:, :, cols])
                    dve.wait_ge(zsplit_hi, 2 * (FC * z + f) + 2)
                    if z == 0 and f == FC // 2:
                        dve.wait_ge(vt_turned, A0_UNITS // 2)
                    dve.scalar_tensor_tensor(WBL[:, f, :], WSB[:, f, :], WK[:, z // TOPK, z % TOPK:z % TOPK + 1],
                                             WBH[:, f, :].bitcast(F32), ALU.mult, ALU.subtract).then_inc(zsplit_done, 1)
                elif kind == "zone":
                    s = step[1]
                    dve.wait_ge(act_done, s + 1)
                    if s >= 2:
                        dve.wait_ge(y_done, s - 1)
                    else:
                        dve.wait_ge(pv_done, A0_UNITS // 2)
                    lo_part(HL[s % 2][:, :], HF[s % 2][:, :], HH[s % 2][:, :]).then_inc(hl_ready, 1)
                elif kind == "out":
                    _, stage, j = step
                    for i in range(2):
                        key = step + (i,)
                        filled(dve, key)
                        xi = X[:, TT * j + 2 * i:TT * j + 2 * i + 2, :]
                        if stage == FFN0:
                            dve.wait_ge(added, j + 1)
                        dve.tensor_tensor(xi, bank(key).rearrange("p (t d) -> p t d", t=2), xi, ALU.add).then_inc(frees(key), 1)
                elif kind == "turn_mix":
                    j = step[1]
                    for c in range(KC):
                        key = step + (c,)
                        dve.wait_ge(mix_hi, KC * j + c + 1)
                        lo_part(XL[:, j, c, :], bank(key), XH[:, j, c, :]).then_inc(frees(key), 1)
                elif kind == "project":
                    j = step[1]
                    for i in range(2):
                        key = step + (i,)
                        filled(dve, key)
                        xi = X[:, TT * j + 2 * i:TT * j + 2 * i + 2, :]
                        dve.scalar_tensor_tensor(xi, bank(key).rearrange("p (t d) -> p t d", t=2), TG[:, 1:2], xi,
                                                 ALU.mult, ALU.add).then_inc(frees(key), 1)
                elif kind == "ffn_split":
                    i = step[1]
                    dve.wait_ge(fsplit_hi, i + 1)
                    src = WI[i % 2][:, :].rearrange("p (c n) -> p c n", c=KC if i < 2 else HC)
                    lo_part((WGL, WUL, WNL)[i][:, :, :], src, (WGH, WUH, WNH)[i][:, :, :]).then_inc(fsplit_done, 1)
                elif kind in ("gated", "gated_end"):
                    s = step[1] if kind == "gated" else GSTEPS
                    if kind == "gated":
                        dve.wait_ge(silu_done, s + 1)
                        if s >= 2:
                            dve.wait_ge(ghl_ready, s - 1)
                        else:
                            dve.wait_ge(pv_done, ALL_UNITS // 2)
                        dve.scalar_tensor_tensor(HF[s % 2][:, :], SC[:, s % 2, 1, :], DEQ, SG[s % 2][:, :],
                                                 ALU.mult, ALU.mult).then_inc(hf_ready, 1)
                    if s:
                        dve.wait_ge(ghh_ready, s)
                        if s >= 3:
                            dve.wait_ge(gy_done, s - 2)
                        lo_part(HL[(s - 1) % 2][:, :], HF[(s - 1) % 2][:, :], HH[(s - 1) % 2][:, :]).then_inc(ghl_ready, 1)

        @block.tensor
        def _(pe):
            def fill(key):
                n = aux[key]
                if n >= 2:
                    pe.wait_ge(aux_free[n % 2], n // 2)
                return AUX[:, n % 2, :]

            def product(ps, terms, start=True, stop=True):
                passes = [p for lh, ll, rh, rl in terms for p in ((lh, rh), (lh, rl), (ll, rh))]
                for i, (lhs, rhs) in enumerate(passes):
                    ins = pe.matmul(ps, lhs, rhs, start=start and i == 0, stop=stop and i == len(passes) - 1)
                return ins

            def attend_values(q):
                a = 1 if q >= A0_UNITS // 2 else 0
                j, u = divmod(2 * q - (A0_UNITS if a else 0), units[a])
                pe.wait_ge(exp_done, 2 * q + 2)
                if q == 0:
                    pe.wait_ge(pv_set, 1)
                if q >= 2:
                    pe.wait_ge(pv_out, q - 1)
                for i in range(4):
                    h = 2 * u + i
                    ins = pe.matmul(PV[32 * i:32 * i + DV + 1, q % 2, :], V[a][0:S, j // 2, h // 2 if a == 0 else h, :],
                                    probs(2 * q + i // 2)[0:S, i % 2, :], start=True, stop=True)
                ins.then_inc(pv_done, 1)

            def attend_turn(q):
                pe.wait_ge(vt_ready, q + 1)
                for t in range(TT):
                    cols = slice(P * t, P * (t + 1))
                    ins = pe.transpose(PV[:, q % 2, cols], VT[1 if q >= A0_UNITS // 2 else 0][:, q % 2, cols], ident[:, :])
                ins.then_inc(vt_turned, 1)

            def zone_out(s):
                z, nt, f = s // PER, s % PER // FC, s % FC
                pe.wait_ge(hl_ready, s + 1)
                first, last = z % TOPK == 0 and f == 0, z % TOPK == TOPK - 1 and f == FC - 1
                if first and z:
                    pe.wait_ge(ys_ready, nt + 1)
                for c in range(KC):
                    cols = slice(P * c, P * (c + 1))
                    ins = product(SC[:, nt, c, :], [(WBH[:, f, cols], WBL[:, f, cols], HH[s % 2][:, :], HL[s % 2][:, :])],
                                  start=first, stop=last)
                ins.then_inc(y_done, 1)

            def gated_out(s):
                j, f = divmod(s, HC)
                pe.wait_ge(ghl_ready, s + 1)
                if f == 0:
                    if j:
                        pe.wait_ge(ys_ready, J + j)
                    else:
                        pe.wait_ge(fsplit_done, 3)
                        pe.wait_ge(pv_out, ALL_UNITS // 2)
                for c in range(KC):
                    cols = slice(P * c, P * (c + 1))
                    ins = product(PV[:, c, :], [(WNH[:, f, cols], WNL[:, f, cols], HH[s % 2][:, :], HL[s % 2][:, :])],
                                  start=f == 0, stop=f == HC - 1)
                ins.then_inc(gy_done, 1)

            pe.wait_ge(const_in, 32)
            for step in PLAN:
                kind = step[0]
                if kind == "turn":
                    pe.wait_ge(xn_ready, order[step] + 1)
                    for c in range(KC):
                        ps = fill(step + (c,))
                        for t in range(TT):
                            ins = pe.transpose(ps[:, P * t:P * (t + 1)], XN[:, t, P * c:P * (c + 1)], ident[:, :])
                        ins.then_inc(aux_ready, 1)
                elif kind == "keys":
                    a = step[1]
                    pe.wait_ge(split_done, a + 2)
                    for i in range(3):
                        ps = fill(step + (i,))
                        for g in range(3 * i, min(3 * i + 3, G)):
                            terms = [(WDH[:, c, g, :, :].rearrange("p q r -> p (q r)"), WDL[:, c, g, :, :].rearrange("p q r -> p (q r)"),
                                      CH[:, c, :], CL[:, c, :]) for c in range(KC)]
                            ins = product(ps[0:ROWS, (g - 3 * i) * B * S:(g - 3 * i + 1) * B * S], terms)
                        ins.then_inc(aux_ready, 1)
                    vh, vl = (WVH, WVL) if a == 0 else (WQ1H, WQ1L)
                    for b in range(B):
                        ps = fill(step + (3 + b,))
                        cols = slice(b * S, (b + 1) * S)
                        product(ps[0:S, 0:D], [(CH[:, c, cols], CL[:, c, cols], vh[:, c, :], vl[:, c, :])
                                               for c in range(KC)]).then_inc(aux_ready, 1)
                elif kind == "query":
                    _, a, j = step
                    for c in range(KC):
                        used(pe, ("turn", ATT1 if a else ATT0, j, c))
                    wh, wl = (WQ1H, WQ1L) if a else (WQ0H, WQ0L)
                    if a == 0:
                        pe.wait_ge(split_done, 1)
                    for c in range(KC):
                        cols = slice(P * c, P * (c + 1))
                        product(fill(step + (c,)), [(wh[:, k, cols], wl[:, k, cols], XH[:, j, k, :], XL[:, j, k, :])
                                                    for k in range(KC)]).then_inc(aux_ready, 1)
                elif kind == "max":
                    _, a, j, t, u = step
                    n = J * a + j
                    half = units[a] // 4
                    if t == 0 and u % half == 0:
                        pe.wait_ge(q_moved[n % 2][u // half], 16 * 12 * (n // 2 + 1))
                        pe.wait_ge(ka_ready, a + 1)
                    ps = fill(step + (0,))
                    for i in range(4 // NS[a]):
                        g = u * (4 // NS[a]) + i
                        n_cols = NS[a] * S
                        ins = pe.matmul(ps[:, i * n_cols:(i + 1) * n_cols], QG[n % 2][0:ROWS, g, P * t:P * (t + 1)],
                                        KA[a][0:ROWS, j // 2, NS[a] * g:NS[a] * (g + 1), :].rearrange("p h n -> p (h n)"),
                                        start=True, stop=True)
                    ins.then_inc(aux_ready, 1)
                elif kind == "negmax":
                    _, a, j = step
                    last = 8 if a == 0 else 4
                    for u in (last - 2, last - 1):
                        used(pe, ("max", a, j, TT - 1, u, 0))
                    ps = fill(step + (0,))
                    for t in range(TT):
                        ins = pe.transpose(ps[0:HEADS[a], P * t:P * (t + 1)], NM[:, (J * a + j) % 2, t, 0:HEADS[a]], ident[:, :])
                    ins.then_inc(aux_ready, 1)
                elif kind == "attend":
                    _, a, j, u = step
                    n, m = unit(a, j, u), J * a + j
                    if u == 0:
                        pe.wait_ge(m_moved[m % 2], 16 * G * (m // 2 + 1))
                    if a == 1 and n < A0_UNITS + 2:
                        pe.wait_ge(ys_ready, 3 + n - A0_UNITS)
                    if n >= 2:
                        pe.wait_ge(exp_done, n - 1)
                    rows = ROWS + NS[a]
                    for i in range(2):
                        h = 2 * u + i
                        ins = pe.matmul(SC[0:S, n % 2, i, :], KA[a][0:rows, j // 2, h, :], QG[m % 2][0:rows, h // NS[a], :],
                                        start=True, stop=True)
                    ins.then_inc(sc_ready, 1)
                elif kind == "quad_turn":
                    _, a, j, u = step
                    if unit(a, j, u) - 4 >= unit(a, 0, 0):
                        attend_turn(unit(a, j, u) // 2 - 2)
                elif kind == "quad_values":
                    _, a, j, u = step
                    if unit(a, j, u) - 2 >= unit(a, 0, 0):
                        attend_values(unit(a, j, u) // 2 - 1)
                elif kind == "attend_end":
                    end = (ALL_UNITS if step[1] else A0_UNITS) // 2
                    attend_turn(end - 2)
                    attend_values(end - 1)
                    attend_turn(end - 1)
                elif kind == "route":
                    b = step[1]
                    pe.wait_ge(wo_in, 32)
                    pe.wait_ge(small_in, 16 * SMALL)
                    key = step + (0,)
                    ps = fill(key)
                    cols = [(c, 2 * b + i) for c in range(KC) for i in range(2)]
                    for c in range(KC):
                        used(pe, ("turn", FFN0, 2 * b + 1, c))
                    for i, (c, j) in enumerate(cols):
                        ins = pe.matmul(ps[0:RH, 0:1], W1[:, c, :], POOLED[:, c, j:j + 1], start=i == 0, stop=i == len(cols) - 1)
                    ins.then_inc(aux_ready, 1)
                    used(pe, key)
                    pe.matmul(fill(step + (1,))[:, 0:NZ], RHID[:, b:b + 1].to_broadcast([RH, P]), W2[:, :],
                              start=True, stop=True).then_inc(aux_ready, 1)
                elif kind == "zone":
                    s = step[1]
                    z, nt, f = s // PER, s % PER // FC, s % FC
                    j = 2 * (z // TOPK) + nt
                    if z % TOPK == 0 and f == 0:
                        for c in range(KC):
                            used(pe, ("turn", FFN0, j, c))
                    if nt == 0:
                        pe.wait_ge(zsplit_done, FC * z + f + 1)
                    if s >= 2:
                        pe.wait_ge(act_done, s - 1)
                    else:
                        pe.wait_ge(pv_out, A0_UNITS // 2)
                    cols = slice(P * f, P * (f + 1))
                    product(PV[:, s % 2, :], [(WAH[:, c, cols], WAL[:, c, cols], XH[:, j, c, :], XL[:, j, c, :])
                                              for c in range(KC)]).then_inc(h_ready, 1)
                    if s >= LAG:
                        zone_out(s - LAG)
                elif kind == "zone_end":
                    for s in range(ZSTEPS - LAG, ZSTEPS):
                        zone_out(s)
                elif kind == "out":
                    pe.wait_ge(ys_ready, order[step] + 1)
                    for i in range(2):
                        ps = fill(step + (i,))
                        for t in (2 * i, 2 * i + 1):
                            for c in range(KC):
                                at_c = D * (t % 2) + P * c
                                ins = pe.transpose(ps[:, at_c:at_c + P], YS[:, c, P * t:P * (t + 1)], ident[:, :])
                        ins.then_inc(aux_ready, 1)
                elif kind == "turn_mix":
                    j = step[1]
                    pe.wait_ge(mixed, J + j + 1)
                    for c in range(KC):
                        ps = fill(step + (c,))
                        for t in range(TT):
                            ins = pe.transpose(ps[:, P * t:P * (t + 1)], MIX[:, t, P * c:P * (c + 1)], ident[:, :])
                        ins.then_inc(aux_ready, 1)
                elif kind == "project":
                    j = step[1]
                    pe.wait_ge(wo_done, 1)
                    for c in range(KC):
                        used(pe, ("turn_mix", j, c))
                    for i in range(2):
                        ps = fill(step + (i,))
                        for t in (2 * i, 2 * i + 1):
                            rows = slice(P * t, P * (t + 1))
                            ins = product(ps[:, D * (t % 2):D * (t % 2 + 1)],
                                          [(XH[:, j, k, rows], XL[:, j, k, rows], WOH[:, k, :], WOL[:, k, :]) for k in range(KC)])
                        ins.then_inc(aux_ready, 1)
                elif kind == "gated":
                    s = step[1]
                    j, f = divmod(s, HC)
                    if f == 0:
                        pe.wait_ge(fsplit_done, 2)
                        for c in range(KC):
                            used(pe, ("turn", FFN1, j, c))
                    if s >= 2:
                        pe.wait_ge(hf_ready, s - 1)
                    else:
                        pe.wait_ge(exp_done, ALL_UNITS)
                    cols = slice(P * f, P * (f + 1))
                    for i, (wh, wl) in enumerate(((WGH, WGL), (WUH, WUL))):
                        ins = product(SC[:, s % 2, i, :], [(wh[:, c, cols], wl[:, c, cols], XH[:, j, c, :], XL[:, j, c, :])
                                                           for c in range(KC)])
                    ins.then_inc(g_ready, 1)
                    if s >= LAG:
                        gated_out(s - LAG)
                elif kind == "gated_end":
                    for s in range(GSTEPS - LAG, GSTEPS):
                        gated_out(s)


def kernel(**inputs):
    import numpy as np
    import concourse.bacc as bacc
    from concourse.bass_utils import run_bass_kernel_spmd as run

    x = np.asarray(inputs["x"])
    shape = x.shape
    tiles = x.reshape(J, TT, P, D).transpose(0, 2, 1, 3)
    pick = np.zeros((P, sum(NS)), np.float32)
    for a in range(2):
        for s in range(NS[a]):
            size = 32 // NS[a]
            for q in range(3):
                pick[32 * q + size * s:32 * q + size * (s + 1), s + a * NS[0]] = 1.0
            pick[ROWS + s, s + a * NS[0]] = 1.0
    bq = np.asarray(inputs["L1_xattn_bq"])
    arrays = {
        "x": tiles,
        "ctx_t": np.asarray(inputs["ctx_1024"]).reshape(B * S, D).T,
        "g_x": inputs["g_xattn"], "g_f": inputs["g_ffn"],
        "wq0": np.asarray(inputs["L0_xattn_Wq"]).T, "wk0": np.asarray(inputs["L0_xattn_Wk"]).T,
        "wv0": np.asarray(inputs["L0_xattn_Wv"]).T,
        "lq1": inputs["L0_xattn_lambda_q1"], "lq2": inputs["L0_xattn_lambda_q2"],
        "lk1": inputs["L0_xattn_lambda_k1"], "lk2": inputs["L0_xattn_lambda_k2"],
        "w1": inputs["L0_ffn_W1"], "b1": inputs["L0_ffn_b1"], "w2": inputs["L0_ffn_W2"], "b2": inputs["L0_ffn_b2"],
        "wa": inputs["L0_ffn_Wa"], "wb": inputs["L0_ffn_Wb"],
        "wq1": inputs["L1_xattn_Wq"], "bq": bq,
        "bq_c": bq.reshape(KC, P).T, "bq_g": np.tile(bq.reshape(G, 32).T, (3, 1)),
        "wo": inputs["L1_xattn_Wo"], "bo": inputs["L1_xattn_bo"],
        "wg": np.asarray(inputs["L1_ffn_w_gate"]).T, "wu": np.asarray(inputs["L1_ffn_w_up"]).T,
        "wd": np.asarray(inputs["L1_ffn_w_down"]).T,
        "ident": np.eye(P, dtype=np.float32), "pick": pick,
    }
    nc = bacc.Bacc("TRN2", target_bir_lowering=False, num_devices=1)
    fed, args = {}, []
    for name, a in arrays.items():
        a = np.ascontiguousarray(a)
        fed[f"in_{name}"] = a
        args.append(nc.dram_tensor(f"in_{name}", a.shape, mybir.dt.from_np(a.dtype), kind="ExternalInput").ap())
    args.append(nc.dram_tensor("out_x", tiles.shape, F32, kind="ExternalOutput").ap())
    flamingo(nc, *args)
    r = run(nc, [fed], core_ids=[0])
    got = np.asarray(r.results[0]["out_x"])
    return got.transpose(0, 2, 1, 3).reshape(shape)
```
